# Optimizing a Trainium2 kernel written in Bass

```python
import numpy as np
import jax
import jax.numpy as jnp

def _softmax(x, axis=-1):
    return jax.nn.softmax(x, axis=axis)

def _gelu(x):
    return jax.nn.gelu(x, approximate=True)

def _silu(x):
    return jax.nn.silu(x)

def _sigmoid(x):
    return jax.nn.sigmoid(x)

def _layernorm(x, axis=-1, eps=1e-05):
    m = jnp.mean(x, axis=axis, keepdims=True)
    v = jnp.var(x, axis=axis, keepdims=True)
    return (x - m) / jnp.sqrt(v + eps)

def _scatter_add(tgt, idx, src, axis=0):
    return tgt.at[idx].add(src)

def _segment_sum(src, seg, n):
    return jax.ops.segment_sum(src, seg, n)
kernel_name = 'mk_gnn_ffn_d1_gnn_r32_0107b0'

def setup_inputs(seed: int=0):
    np.random.seed(seed)
    _w = jnp.asarray

    def _rec_inputs():
        import jax
        import jax.numpy as jnp
        _gk = jax.random.key(seed)
        x = -8.776e-05 + 1 * jax.random.normal(jax.random.fold_in(_gk, 1), (625, 256), jnp.float32)
        src = jax.random.randint(jax.random.fold_in(_gk, 2), (20000,), 0, 625, jnp.int32)
        dst = jnp.minimum((625 * jax.random.uniform(jax.random.fold_in(_gk, 3), (20000,)) ** 2.0).astype(jnp.int32), 19999)
        _o = jnp.argsort(dst, stable=True)
        src = src[_o]
        dst = dst[_o]
        return (x, src, dst)
    x, src, dst = _rec_inputs()

    def _L0_gnn_setup():
        import jax, jax.numpy as jnp
        import numpy as np
        N = 625
        E = 10000
        DIN = 256
        DOUT = 256
        L = 3

        def _edge_conv(x, src, dst, W, b):
            xi = x[dst]
            xj = x[src]
            m = jnp.concatenate([xi, xj - xi], axis=-1) @ W + b
            s = jax.ops.segment_sum(m, dst, num_segments=N)
            cnt = jax.ops.segment_sum(jnp.ones((dst.shape[0],), m.dtype), dst, num_segments=N)
            return s / jnp.maximum(cnt, 1.0)[:, None]
        key = jax.random.key(seed)
        ks = jax.random.split(key, 4 + 2 * L)
        x = jax.random.normal(ks[0], (N, DIN), dtype=jnp.float32)
        edge_index = jax.random.randint(ks[1], (2, E), 0, N, dtype=jnp.int64)
        scale = 0.05
        inp = {'x': x, 'edge_index': edge_index}
        din = DIN
        for l in range(L):
            inp[f'W{l}'] = jax.random.normal(ks[2 + l], (2 * din, DOUT), dtype=jnp.float32) * scale
            inp[f'b{l}'] = jnp.zeros((DOUT,), dtype=jnp.float32)
            din = DOUT
        cat_dim = DIN + L * DOUT
        inp['Wf'] = jax.random.normal(ks[2 + L], (cat_dim, DOUT), dtype=jnp.float32) * scale
        inp['bf'] = jnp.zeros((DOUT,), dtype=jnp.float32)
        return inp
    _L0_gnn_all = _L0_gnn_setup()
    _L0_gnn_in = {k: v for k, v in _L0_gnn_all.items() if k in ('W0', 'b0', 'W1', 'b1', 'W2', 'b2', 'Wf', 'bf')}
    del _L0_gnn_all

    def _L0_ffn_setup():
        import jax, jax.numpy as jnp
        import numpy as np
        B, S, D, E, H, K = (4, 128, 256, 8, 512, 2)
        key = jax.random.key(seed)
        ks = jax.random.split(key, 6)
        x = jax.random.normal(ks[0], (B, S, D), jnp.float32)
        Wg = jax.random.normal(ks[1], (D, E), jnp.float32) * 0.02
        bg = jnp.zeros((E,), jnp.float32)
        W1 = jax.random.normal(ks[2], (E, D, H), jnp.float32) * 0.02
        b1 = jnp.zeros((E, H), jnp.float32)
        W2 = jax.random.normal(ks[3], (E, H, D), jnp.float32) * 0.02
        b2 = jnp.zeros((E, D), jnp.float32)
        return {'x': x, 'Wg': Wg, 'bg': bg, 'W1': W1, 'b1': b1, 'W2': W2, 'b2': b2}
    _L0_ffn_all = _L0_ffn_setup()
    _L0_ffn_in = {k: v for k, v in _L0_ffn_all.items() if k in ('Wg', 'bg', 'W1', 'b1', 'W2', 'b2')}
    del _L0_ffn_all
    return {'x': x, 'src': src, 'dst': dst, 'L0_gnn_W0': _L0_gnn_in['W0'], 'L0_gnn_b0': _L0_gnn_in['b0'], 'L0_gnn_W1': _L0_gnn_in['W1'], 'L0_gnn_b1': _L0_gnn_in['b1'], 'L0_gnn_W2': _L0_gnn_in['W2'], 'L0_gnn_b2': _L0_gnn_in['b2'], 'L0_gnn_Wf': _L0_gnn_in['Wf'], 'L0_gnn_bf': _L0_gnn_in['bf'], 'L0_ffn_Wg': _L0_ffn_in['Wg'], 'L0_ffn_bg': _L0_ffn_in['bg'], 'L0_ffn_W1': _L0_ffn_in['W1'], 'L0_ffn_b1': _L0_ffn_in['b1'], 'L0_ffn_W2': _L0_ffn_in['W2'], 'L0_ffn_b2': _L0_ffn_in['b2']}

def reference(x, src, dst, L0_gnn_W0, L0_gnn_b0, L0_gnn_W1, L0_gnn_b1, L0_gnn_W2, L0_gnn_b2, L0_gnn_Wf, L0_gnn_bf, L0_ffn_Wg, L0_ffn_bg, L0_ffn_W1, L0_ffn_b1, L0_ffn_W2, L0_ffn_b2):
    import jax
    import jax.numpy as jnp

    def _L0_gnn_ref(x, edge_index, W0, b0, W1, b1, W2, b2, Wf, bf):
        import jax, jax.numpy as jnp
        import numpy as np
        N = 625
        E = 10000
        DIN = 256
        DOUT = 256
        L = 3

        def _edge_conv(x, src, dst, W, b):
            xi = x[dst]
            xj = x[src]
            m = jnp.concatenate([xi, xj - xi], axis=-1) @ W + b
            s = jax.ops.segment_sum(m, dst, num_segments=N)
            cnt = jax.ops.segment_sum(jnp.ones((dst.shape[0],), m.dtype), dst, num_segments=N)
            return s / jnp.maximum(cnt, 1.0)[:, None]
        src, dst = (edge_index[0], edge_index[1])
        xs = [x]
        h = x
        for W, b in ((W0, b0), (W1, b1), (W2, b2)):
            h = jax.nn.relu(_edge_conv(h, src, dst, W, b))
            xs.append(h)
        cat = jnp.concatenate(xs, axis=-1)
        return cat @ Wf + bf

    def _L0_ffn_ref(x, Wg, bg, W1, b1, W2, b2):
        import jax, jax.numpy as jnp
        import numpy as np
        B, S, D, E, H, K = (4, 128, 256, 8, 512, 2)
        Bv, Sv, Dv = x.shape
        gate_scores = x @ Wg + bg
        _, idx = jax.lax.top_k(gate_scores, K)
        mask = jax.nn.one_hot(idx, E, dtype=x.dtype).sum(axis=-2)
        xf = x.reshape(-1, Dv)
        mf = mask.reshape(-1, E)
        h = jax.nn.gelu(jnp.einsum('td,edh->teh', xf, W1) + b1[None], approximate=False)
        y = jnp.einsum('teh,ehd->ted', h, W2) + b2[None]
        out = jnp.einsum('ted,te->td', y, mf)
        return out.reshape(Bv, Sv, Dv)
    edge_index = jnp.stack([src, dst])
    x = x + _L0_gnn_ref(_layernorm(x, axis=-1), edge_index, L0_gnn_W0, L0_gnn_b0, L0_gnn_W1, L0_gnn_b1, L0_gnn_W2, L0_gnn_b2, L0_gnn_Wf, L0_gnn_bf)
    x = x + _L0_ffn_ref(_layernorm(x, axis=-1)[None], L0_ffn_Wg, L0_ffn_bg, L0_ffn_W1, L0_ffn_b1, L0_ffn_W2, L0_ffn_b2)[0]
    return x

_drawn_inputs = setup_inputs


def setup_inputs(seed=0):
    import zlib

    import numpy as np

    out = dict(_drawn_inputs(seed))
    spreads = {'L0_gnn_b0': (0.0, 0.1),
     'L0_gnn_b1': (0.0, 0.1),
     'L0_gnn_b2': (0.0, 0.1),
     'L0_gnn_bf': (0.0, 0.1),
     'L0_ffn_bg': (0.0, 0.1),
     'L0_ffn_b1': (0.0, 0.346),
     'L0_ffn_b2': (0.0, 0.1)}
    factors = {}
    for name, (base, spread) in spreads.items():
        noise = np.random.default_rng([zlib.crc32(name.encode()), seed]).standard_normal(out[name].shape)
        drawn = base * np.exp(spread * noise) if base else spread * noise
        out[name] = jnp.asarray(drawn.astype(out[name].dtype))
    for name, factor in factors.items():
        out[name] = (out[name] * factor).astype(out[name].dtype)
    return out
```

```python
import concourse.bass as bass
from concourse import mybir
from contextlib import ExitStack
import numpy as np

NODES = 625
EDGES = 20000
D = 256
LEVELS = 3
EXPERTS = 8
HID = 512
EPS = 1e-5

P = 128
NT = -(-NODES // P)
NPAD = NT * P
LAST = NODES - (NT - 1) * P
KC = D // P
HC = HID // P

EP = 125
ET = EDGES // EP
EH = 2
EQ = ET // EH
assert EP * ET == EDGES and EQ * EH == ET and EQ <= P

WD = 32
NW = NPAD // WD
GROUPS = NT
WPG = NW // GROUPS
SHIFT = ET
RING = 8

MAX_TILES = (2 * NODES + EXPERTS * (P - 1)) // P
MIN_TILES = -(-2 * NODES // P)
AHEAD = 3
SLOT_TILES = MAX_TILES + AHEAD


def build(nc, x, src, dst, W, B, Wf, bf, Wg, bg, W1, b1, W2, b2, out):
    f32, f32r = mybir.dt.float32, mybir.dt.float32r
    bf16, i32, i16, u32 = mybir.dt.bfloat16, mybir.dt.int32, mybir.dt.int16, mybir.dt.uint32
    ALU = mybir.AluOpType
    ACT = mybir.ActivationFunctionType
    AX = mybir.AxisListType
    ds = bass.ds

    ys_dram = nc.dram_tensor("ys_rows", [MAX_TILES * P, D], f32, kind="Internal").ap()

    ctx = ExitStack()
    with ctx:
        def sb(name, shape, dt, scope=ctx):
            return scope.enter_context(nc.sbuf_tensor(name, shape, dt))

        def sem(name):
            return ctx.enter_context(nc.semaphore(name))

        w1_sb = sb("w1_sb", [P, EXPERTS, KC, HID], f32)
        w2_sb = sb("w2_sb", [P, EXPERTS, HC, D], f32)
        wg_sb = sb("wg_sb", [P, KC, EXPERTS], f32)
        bg_row = sb("bg_row", [1, EXPERTS], f32)
        x_sb = sb("x_sb", [P, NT, D], f32)
        x1_sb = sb("x1_sb", [P, NT, D], f32)
        ident = sb("ident", [P, P], f32)
        ones_rowf = sb("ones_rowf", [1, P], f32)
        ones_sq = sb("ones_sq", [P, P], f32r)
        ones_bf = sb("ones_bf", [P, P], bf16)
        tri_bf = sb("tri_bf", [P, P], bf16)
        stats = sb("stats", [P, NT, 6], f32)
        mv = sb("mv", [P, NT, 2], f32)
        std = sb("std", [P, NT], f32)
        rstd = sb("rstd", [P, NT], f32)
        var_eps = sb("var_eps", [P, NT], f32)
        newton = sb("newton", [P, NT], f32)
        iota_lo = sb("iota_lo", [P, P], i16)

        gnn = ExitStack()
        w_stage = sb("w_stage", [P, 3, KC, D], f32, gnn)
        w_hi = sb("w_hi", [P, 2, KC, 3 * D], f32r, gnn)
        w_lo = sb("w_lo", [P, 2, KC, 3 * D], f32r, gnn)
        w_diff = sb("w_diff", [P, KC, D], f32, gnn)
        b_rows = sb("b_rows", [LEVELS + 1, D], f32, gnn)
        b_hi = sb("b_hi", [LEVELS + 1, D], f32r, gnn)
        b_lo = sb("b_lo", [LEVELS + 1, D], f32r, gnn)
        row_pick = sb("row_pick", [LEVELS + 1, LEVELS + 1, P], f32r, gnn)
        a_f = sb("a_f", [P, NT, P], f32, gnn)
        a_hi = sb("a_hi", [P, NT, NPAD], f32r, gnn)
        a_lo = sb("a_lo", [P, NT, NPAD], f32r, gnn)
        deg = sb("deg", [P, P], f32, gnn)
        rdeg = sb("rdeg", [P, NPAD], f32, gnn)
        dg_f = sb("dg_f", [P, P], f32, gnn)
        dg_hi = sb("dg_hi", [P, NT, P], f32r, gnn)
        dg_lo = sb("dg_lo", [P, NT, P], f32r, gnn)
        ht_f = sb("ht_f", [P, KC, NPAD], f32, gnn)
        ht_hi = sb("ht_hi", [P, KC, NPAD], f32r, gnn)
        ht_lo = sb("ht_lo", [P, KC, NPAD], f32r, gnn)
        ys_hi = sb("ys_hi", [P, NT, 2 * D], f32r, gnn)
        ys_lo = sb("ys_lo", [P, NT, 2 * D], f32r, gnn)
        xn = x1_sb
        src_nat = sb("src_nat", [EQ, EH, EP], i32, gnn)
        dst_nat = sb("dst_nat", [EQ, EH, EP], i32, gnn)
        hi_nat = sb("hi_nat", [EQ, EH, EP], i32, gnn)
        lo_nat = sb("lo_nat", [EQ, EH, EP], i32, gnn)
        edge_nat = sb("edge_nat", [EQ, 2, EH, EP], f32, gnn)
        edge_col = sb("edge_col", [EP, 2, ET], f32, gnn)
        span = sb("span", [EQ, 2, EH], f32, gnn)
        tile_id = sb("tile_id", [EQ, 2, EH], f32, gnn)
        win_lo = sb("win_lo", [EQ, EH, NW], f32, gnn)
        touch_a = sb("touch_a", [EQ, EH, NW], f32, gnn)
        touch = sb("touch", [EQ, EH, NW], f32, gnn)
        reach = sb("reach", [EQ, 2, EH, NW], f32, gnn)
        reach_col = sb("reach_col", [2 * EH * NW, 1], f32, gnn)
        reach_row = sb("reach_row", [1, 2, EH, NW], f32, gnn)
        range_row = sb("range_row", [1, 4, NW], f32, gnn)
        zero_row = sb("zero_row", [1, NW], f32, gnn)
        range_i = sb("range_i", [1, 3, NW], i32, gnn)
        iota_key = sb("iota_key", [P, NT, NPAD], i16, gnn)
        hot_lo = sb("hot_lo", [EP, RING, P], bf16, gnn)
        hot_key = sb("hot_key", [EP, RING, NT, WD], bf16, gnn)
        zeros_bf = sb("zeros_bf", [1, NT * WD], bf16, gnn)
        gnn.close()

        ffn = ExitStack()
        b1_bc = sb("b1_bc", [P, EXPERTS, HID], f32, ffn)
        b2_bc = sb("b2_bc", [P, EXPERTS, D], f32, ffn)
        x2 = sb("x2", [P, NT, D], f32, ffn)
        x2_hi = sb("x2_hi", [P, NT, D], f32r, ffn)
        x2_lo = sb("x2_lo", [P, NT, D], f32r, ffn)
        x2_t = sb("x2_t", [P, KC, NPAD], f32, ffn)
        score = sb("score", [P, NT, EXPERTS], f32, ffn)
        best = sb("best", [P, NT, 8], f32, ffn)
        best_id = sb("best_id", [P, NT, 8], u32, ffn)
        best_f = sb("best_f", [P, NT, 2], f32, ffn)
        iota_e = sb("iota_e", [P, NT, EXPERTS], f32, ffn)
        node_id = sb("node_id", [P, NT], f32, ffn)
        valid = sb("valid", [P, NT], f32, ffn)
        pick = sb("pick", [P, 2, NT, EXPERTS], f32, ffn)
        both = sb("both", [P, NT, EXPERTS], f32, ffn)
        both_bf = sb("both_bf", [P, NT, EXPERTS], bf16, ffn)
        tile_sum = sb("tile_sum", [P, NT + 1, EXPERTS], f32, ffn)
        tiles_i = sb("tiles_i", [P, 2, EXPERTS], i32, ffn)
        tiles_f = sb("tiles_f", [P, EXPERTS], f32, ffn)
        tiles_end = sb("tiles_end", [P, EXPERTS], f32, ffn)
        zeros_e = sb("zeros_e", [P, EXPERTS], f32, ffn)
        slot0 = sb("slot0", [P, EXPERTS], f32, ffn)
        slot = sb("slot", [P, NT, EXPERTS], f32, ffn)
        slot_hot = sb("slot_hot", [P, EXPERTS, NT], f32, ffn)
        slot_pick = sb("slot_pick", [P, 2, NT, EXPERTS], f32, ffn)
        slot_of = sb("slot_of", [P, 2, NT], f32, ffn)
        slot_idx = sb("slot_idx", [P, 2, NT], u32, ffn)
        iota_s = sb("iota_s", [1, SLOT_TILES, EXPERTS], f32, ffn)
        past = sb("past", [1, SLOT_TILES, EXPERTS], f32, ffn)
        owner = sb("owner", [1, SLOT_TILES + 1], f32, ffn)
        owner_i = sb("owner_i", [1, SLOT_TILES + 1], i32, ffn)
        iota_slot = sb("iota_slot", [P, SLOT_TILES, P], i16, ffn)
        hot_slot = sb("hot_slot", [P, NT, P], f32r, ffn)
        xt = sb("xt", [P, KC, P], f32, ffn)
        h_pre = sb("h_pre", [P, HID], f32, ffn)
        h_act = sb("h_act", [P, HID], f32, ffn)
        h_t = sb("h_t", [P, HC, P], f32, ffn)
        y_sb = sb("y_sb", [P, SLOT_TILES, D], f32, ffn)
        y_back = sb("y_back", [P, NT, 2, D], f32, ffn)
        ffn.close()

        bank = [ctx.enter_context(nc.psum_tensor(f"bank{i}", [P, 512], f32)) for i in range(2)]
        cnt_ps = ctx.enter_context(nc.psum_tensor("cnt_ps", [P, 1024], f32))
        bank += [cnt_ps[:, 0:512], cnt_ps[:, 512:1024]]
        bank += [ctx.enter_context(nc.psum_tensor("bank4", [P, 512], f32))]
        g_ps = [ctx.enter_context(nc.psum_tensor(f"g_ps{i}", [P, 512], f32)) for i in range(3)]

        def g_tile(t):
            return g_ps[t // 2][:, (t % 2) * D:(t % 2) * D + D]

        edges_in = sem("edges_in")
        x_in = sem("x_in")
        small_in = sem("small_in")
        w_in = [sem(f"w_in{l}") for l in range(LEVELS + 1)]
        ffn_w_in = sem("ffn_w_in")
        ffn_b_in = sem("ffn_b_in")
        consts = sem("consts")
        x_zeroed = sem("x_zeroed")
        pool_chain = sem("pool_chain")
        w_split = sem("w_split")
        b_split = sem("b_split")
        ffn_consts = sem("ffn_consts")
        vec = sem("vec")
        edge_nat_done = sem("edge_nat_done")
        reach_done = sem("reach_done")
        edge_t_done = sem("edge_t_done")
        edge_col_done = sem("edge_col_done")
        reach_t_done = sem("reach_t_done")
        reach_col_done = sem("reach_col_done")
        reach_row_ps = sem("reach_row_ps")
        ranges_ready = sem("ranges_ready")
        var_ready = sem("var_ready")
        std_ready = sem("std_ready")
        xn_ready = sem("xn_ready")
        xn_t_done = sem("xn_t_done")
        ht_hi_done = sem("ht_hi_done")
        ht_f_done = sem("ht_f_done")
        ht_ready = sem("ht_ready")
        pair_ready = sem("pair_ready")
        pair_free = sem("pair_free")
        window_done = sem("window_done")
        window_free = sem("window_free")
        a_hi_done = sem("a_hi_done")
        a_lo_done = sem("a_lo_done")
        cnt_done = sem("cnt_done")
        dg_done = sem("dg_done")
        ys_done = sem("ys_done")
        ys_hi_done = sem("ys_hi_done")
        ys_ready = sem("ys_ready")
        z_done = sem("z_done")
        g_done = sem("g_done")
        x1_ready = sem("x1_ready")
        x2_ready = sem("x2_ready")
        x2_t_ps = sem("x2_t_ps")
        x2_t_ready = sem("x2_t_ready")
        score_ps = sem("score_ps")
        both_ready = sem("both_ready")
        prefix_ps = sem("prefix_ps")
        route_ready = sem("route_ready")
        hot_ready = sem("hot_ready")
        gathered = sem("gathered")
        xt_ready = sem("xt_ready")
        up_done = sem("up_done")
        pre_ready = sem("pre_ready")
        act_ready = sem("act_ready")
        t_done = sem("t_done")
        h_t_ready = sem("h_t_ready")
        down_done = sem("down_done")
        y_ready = sem("y_ready")
        y_stored = sem("y_stored")
        rows_filled = sem("rows_filled")
        rows_stored = sem("rows_stored")
        y_in = [sem(f"y_in{t}") for t in range(NT)]
        out_ready = sem("out_ready")
        out_stored = sem("out_stored")

        block = ctx.enter_context(nc.Block())

        x_rows = x[0:(NT - 1) * P, :].rearrange("(t p) d -> p t d", p=P)
        HALVES = [(0, 3 * P), (3 * P, NPAD)]
        Z_OUT = [(h, c) for h in range(2) for c in range(KC)]

        def ys_bank(l, t):
            return 4 if l == 0 or t % 2 == 0 else 0

        def gather_ps():
            return bank[0][:, 0:D].rearrange("p (k s) -> p k s", k=KC)

        def load_range(eng, w):
            first = eng.value_load(range_i[0:1, 0, ds(w, 1)], min_val=0, max_val=ET - 1)
            end = eng.value_load(range_i[0:1, 1, ds(w, 1)], min_val=1, max_val=ET)
            shift = eng.value_load(range_i[0:1, 2, ds(w, 1)], min_val=1, max_val=SHIFT + NW * ET)
            return first, end, shift

        @block.sync
        def _(sp):
            sp.dma_start(dst_nat[:], dst.rearrange("(j q e) -> q j e", j=EH, e=EP)).then_inc(edges_in, 16)
            sp.dma_start(src_nat[:], src.rearrange("(j q e) -> q j e", j=EH, e=EP)).then_inc(edges_in, 16)
            sp.wait_ge(x_zeroed, 1)
            sp.dma_start(x_sb[:, 0:NT - 1, :], x_rows).then_inc(x_in, 16)
            sp.dma_start(x_sb[0:LAST, NT - 1, :], x[(NT - 1) * P:NODES, :]).then_inc(x_in, 16)
            for i, b in enumerate(B + [bf]):
                sp.dma_start(b_rows[i:i + 1, :], b.unsqueeze(0)).then_inc(small_in, 16)
            for l in range(LEVELS + 1):
                if l:
                    sp.wait_ge(w_split, l)
                if l < LEVELS:
                    sp.dma_start(w_stage[:, 0:2, :, :],
                                 W[l].rearrange("(h k p) d -> p h k d", h=2, k=KC)).then_inc(w_in[l], 16)
                sp.dma_start(w_stage[:, 2, :, :],
                             Wf[l * D:(l + 1) * D, :].rearrange("(k p) d -> p k d", k=KC)).then_inc(w_in[l], 16)
            sp.dma_start(wg_sb[:], Wg.rearrange("(k p) e -> p k e", k=KC)).then_inc(ffn_w_in, 16)
            sp.dma_start(bg_row[:], bg.unsqueeze(0)).then_inc(ffn_w_in, 16)
            for e in range(EXPERTS):
                sp.dma_start(w1_sb[:, e, :, :], W1[e].rearrange("(k p) h -> p k h", k=KC)).then_inc(ffn_w_in, 16)
                sp.dma_start(w2_sb[:, e, :, :], W2[e].rearrange("(k p) d -> p k d", k=HC)).then_inc(ffn_w_in, 16)
            sp.dma_start(ys_dram[MIN_TILES * P:, :],
                         W1.rearrange("e k (a d) -> (e k a) d", d=D)[0:(MAX_TILES - MIN_TILES) * P, :])\
                .then_inc(rows_filled, 16)
            sp.wait_ge(x1_ready, NT)
            for e in range(EXPERTS):
                sp.dma_start(b1_bc[:, e, :], b1[e].partition_broadcast(P)).then_inc(ffn_b_in, 16)
            sp.dma_start(b2_bc[:], b2.rearrange("e d -> (e d)").partition_broadcast(P)
                         .rearrange("p (e d) -> p e d", e=EXPERTS)).then_inc(ffn_b_in, 16)
            sp.wait_ge(route_ready, 1)
            tiles = sp.value_load(owner_i[0:1, SLOT_TILES:SLOT_TILES + 1], min_val=MIN_TILES, max_val=MAX_TILES)
            sp.wait_ge(rows_filled, 16)
            with sp.Fori(0, tiles) as s:
                sp.wait_ge(y_ready, s + 1)
                sp.dma_start(ys_dram[ds(s * P, P), :], y_sb[:, ds(s, 1), :]).then_inc(y_stored, 16)
            for t in range(NT):
                rows = P if t < NT - 1 else LAST
                sp.wait_ge(out_ready, t + 1)
                sp.dma_start(out[t * P:t * P + rows, :], x1_sb[0:rows, t, :]).then_inc(out_stored, 16)
            sp.wait_ge(out_stored, 16 * NT)

        @block.gpsimd
        def _(pool):
            n = [0]

            def chain(ins):
                n[0] += 1
                ins.then_inc(pool_chain, 1)
                pool.wait_ge(pool_chain, n[0])

            pool.memset(x_sb[:, NT - 1, :], 0.0).then_inc(x_zeroed, 1)
            chain(pool.memset(ident[:], 0.0))
            pool.affine_select(out=ident[:], in_=ident[:], compare_op=ALU.not_equal, fill=1.0, base=0,
                               pattern=[[-1, P]], channel_multiplier=1).then_inc(consts, 1)
            pool.iota(iota_lo[:], pattern=[[1, P]], base=0, channel_multiplier=0,
                      allow_small_or_imprecise_dtypes=True).then_inc(consts, 1)
            pool.iota(win_lo[:], pattern=[[0, EH], [WD, NW]], base=0, channel_multiplier=0,
                      allow_small_or_imprecise_dtypes=True).then_inc(consts, 1)
            pool.iota(tile_id[:, 0, :], pattern=[[EQ, EH]], base=1, channel_multiplier=1,
                      allow_small_or_imprecise_dtypes=True).then_inc(consts, 1)
            pool.iota(tile_id[:, 1, :], pattern=[[-EQ, EH]], base=ET, channel_multiplier=-1,
                      allow_small_or_imprecise_dtypes=True).then_inc(consts, 1)
            pool.iota(iota_key[:], pattern=[[NPAD, NT], [1, NPAD]], base=0, channel_multiplier=0,
                      allow_small_or_imprecise_dtypes=True).then_inc(consts, 1)
            pool.memset(zeros_bf[:], 0.0).then_inc(consts, 1)
            pool.memset(zero_row[:], 0.0).then_inc(consts, 1)
            pool.memset(ones_rowf[:], 1.0).then_inc(consts, 1)
            pool.memset(ones_sq[:].bitcast(f32), 1.0).then_inc(consts, 1)
            pool.memset(ones_bf[:], 1.0).then_inc(consts, 1)
            chain(pool.memset(tri_bf[:], 0.0))
            pool.affine_select(out=tri_bf[:], in_=tri_bf[:], compare_op=ALU.is_ge, fill=1.0, base=0,
                               pattern=[[-1, P]], channel_multiplier=1).then_inc(consts, 1)
            pool.wait_ge(consts, 1)
            pool.tensor_copy(row_pick[:], ident[0:LEVELS + 1, 0:LEVELS + 1].unsqueeze(2)
                             .broadcast_to((LEVELS + 1, LEVELS + 1, P))).then_inc(b_split, 1)
            pool.wait_ge(small_in, 16 * (LEVELS + 1))
            chain(pool.tensor_copy(b_hi[:], b_rows[:]))
            pool.tensor_tensor(b_lo[:], b_rows[:], b_hi[:].bitcast(f32), ALU.subtract).then_inc(b_split, 1)

            def split_weights(l):
                r = l % 2
                pool.wait_ge(w_in[l], 32 if l < LEVELS else 16)
                if l >= 2:
                    pool.wait_ge(z_done if l - 2 < LEVELS else g_done, 4 * (l - 1))
                parts = [(2, w_stage[:, 2, :, :])]
                if l < LEVELS:
                    chain(pool.tensor_tensor(w_diff[:], w_stage[:, 0, :, :], w_stage[:, 1, :, :], ALU.subtract))
                    parts = [(0, w_stage[:, 1, :, :]), (1, w_diff[:]), (2, w_stage[:, 2, :, :])]
                for i, part in parts:
                    pool.tensor_copy(w_hi[:, r, :, i * D:(i + 1) * D], part).then_inc(pool_chain, 1)
                    n[0] += 1
                pool.wait_ge(pool_chain, n[0])
                for i, part in parts:
                    pool.tensor_tensor(w_lo[:, r, :, i * D:(i + 1) * D], part,
                                       w_hi[:, r, :, i * D:(i + 1) * D].bitcast(f32), ALU.subtract)\
                        .then_inc(pool_chain, 1)
                    n[0] += 1
                pool.wait_ge(pool_chain, n[0])
                pool.sem_inc(w_split, 1)

            def split_group(g):
                pool.wait_ge(a_hi_done, WPG * (g + 1))
                pool.tensor_tensor(a_lo[:, :, g * P:(g + 1) * P], a_f[:],
                                   a_hi[:, :, g * P:(g + 1) * P].bitcast(f32), ALU.subtract).then_inc(a_lo_done, 1)

            split_weights(0)
            for g in range(GROUPS):
                split_group(g)
                if g == 0:
                    split_weights(1)
            for l in range(2, LEVELS + 1):
                split_weights(l)

            pool.wait_ge(x1_ready, NT)
            pool.iota(iota_e[:], pattern=[[0, NT], [1, EXPERTS]], base=0, channel_multiplier=0,
                      allow_small_or_imprecise_dtypes=True).then_inc(ffn_consts, 1)
            pool.iota(node_id[:], pattern=[[P, NT]], base=0, channel_multiplier=1,
                      allow_small_or_imprecise_dtypes=True).then_inc(ffn_consts, 1)
            pool.iota(iota_s[:], pattern=[[1, SLOT_TILES], [0, EXPERTS]], base=0, channel_multiplier=0,
                      allow_small_or_imprecise_dtypes=True).then_inc(ffn_consts, 1)
            pool.memset(zeros_e[:], 0.0).then_inc(ffn_consts, 1)
            pool.iota(iota_slot[:], pattern=[[P, SLOT_TILES], [1, P]], base=0, channel_multiplier=0,
                      allow_small_or_imprecise_dtypes=True).then_inc(ffn_consts, 1)
            pool.wait_ge(route_ready, 1)
            tiles = pool.value_load(owner_i[0:1, SLOT_TILES:SLOT_TILES + 1], min_val=MIN_TILES, max_val=MAX_TILES)
            pool.wait_ge(y_stored, tiles * 16)
            pool.sem_inc(rows_stored, 1)
            pool.wait_ge(rows_stored, 1)
            for t in range(NT):
                rows = P if t < NT - 1 else LAST
                for k in range(2):
                    pool.indirect_dma_start(
                        out=y_back[0:rows, t, k, :], out_offset=None, in_=ys_dram,
                        in_offset=bass.IndirectOffsetOnAxis(ap=slot_idx[0:rows, k, t:t + 1], axis=0))\
                        .then_inc(y_in[t], 16)

        @block.scalar
        def _(act):
            act.wait_ge(var_ready, 1)
            act.activation(std[:], var_eps[:], ACT.Sqrt).then_inc(std_ready, 1)
            for i, (h, c) in enumerate(Z_OUT):
                act.wait_ge(ht_f_done, i + 1)
                a, b = HALVES[h]
                act.copy(ht_hi[:, c, a:b], ht_f[:, c, a:b]).then_inc(ht_hi_done, 1)

            def ys_upper(l, t):
                n = l * NT + t
                act.wait_ge(ys_done, n + 1)
                act.copy(ys_hi[:, t, :], bank[ys_bank(l, t)][:, :]).then_inc(ys_hi_done, 1)

            act.sem_inc(window_free, 2)
            for g in range(GROUPS):
                if g >= 1:
                    act.wait_ge(a_lo_done, g)
                with act.Fori(0, WPG // 2) as i:
                    for half in range(2):
                        act.wait_ge(window_done, i * 2 + (g * WPG + half + 1))
                        pane = bank[half][:, 0:NT * WD].rearrange("p (n w) -> p n w", n=NT)
                        act.copy(a_f[:, :, ds(i * (2 * WD) + half * WD, WD)], pane)
                        act.copy(a_hi[:, :, ds(i * (2 * WD) + (g * P + half * WD), WD)], pane)\
                            .then_inc(a_hi_done, 1)
                        act.drain().then_inc(window_free, 1)
                ys_upper(0, g)

            for l in range(LEVELS):
                if l:
                    for t in range(NT):
                        ys_upper(l, t)
                for i, (h, c) in enumerate(Z_OUT):
                    act.wait_ge(ht_f_done, 4 * (l + 1) + i + 1)
                    a, b = HALVES[h]
                    act.copy(ht_hi[:, c, a:b], ht_f[:, c, a:b]).then_inc(ht_hi_done, 1)

            act.wait_ge(var_ready, 2)
            act.activation(std[:], var_eps[:], ACT.Sqrt).then_inc(std_ready, 1)
            for i in range(KC * NT):
                pass
            for s in range(2):
                act.wait_ge(gathered, s + 1)
                if s:
                    act.wait_ge(up_done, s)
                act.copy(xt[:], gather_ps()).then_inc(xt_ready, 1)
                if s == 0:
                    act.wait_ge(pre_ready, 1)
                    act.activation(h_act[:], h_pre[:], ACT.Gelu).then_inc(act_ready, 1)
            act.wait_ge(route_ready, 1)
            tiles = act.value_load(owner_i[0:1, SLOT_TILES:SLOT_TILES + 1], min_val=MIN_TILES, max_val=MAX_TILES)
            with act.Fori(0, tiles) as s:
                act.wait_ge(pre_ready, s + 2)
                act.wait_ge(t_done, s + 1)
                act.activation(h_act[:], h_pre[:], ACT.Gelu).then_inc(act_ready, 1)
                act.wait_ge(gathered, s + 3)
                act.copy(xt[:], gather_ps()).then_inc(xt_ready, 1)

        @block.vector
        def _(dve):
            n = [0]

            def chain(ins):
                n[0] += 1
                ins.then_inc(vec, 1)
                dve.wait_ge(vec, n[0])

            def layer_norm_stats(tile_of, round_):
                for t in range(NT):
                    last = dve.bn_stats(stats[:, t, :], tile_of(t))
                chain(last)
                for t in range(NT):
                    last = dve.bn_aggr(mv[:, t, :], stats[:, t, :])
                chain(last)
                dve.tensor_scalar(var_eps[:], mv[:, :, 1], EPS, None, ALU.add).then_inc(var_ready, 1)
                dve.wait_ge(std_ready, round_)
                chain(dve.reciprocal(rstd[:], std[:]))
                chain(dve.tensor_tensor(newton[:], rstd[:], rstd[:], ALU.mult))
                chain(dve.tensor_tensor(newton[:], newton[:], var_eps[:], ALU.mult))
                chain(dve.tensor_scalar(newton[:], newton[:], -0.5, 1.5, ALU.mult, ALU.add))
                chain(dve.tensor_tensor(rstd[:], rstd[:], newton[:], ALU.mult))

            dve.wait_ge(edges_in, 32)
            dve.tensor_single_scalar(hi_nat[:], src_nat[:], 7, ALU.arith_shift_right).then_inc(vec, 1)
            chain_after = dve.tensor_single_scalar(lo_nat[:], src_nat[:], P - 1, ALU.bitwise_and)
            n[0] += 1
            chain(chain_after)
            dve.tensor_copy(edge_nat[:, 0, :, :], lo_nat[:]).then_inc(edge_nat_done, 1)
            dve.scalar_tensor_tensor(edge_nat[:, 1, :, :], hi_nat[:], float(NPAD), dst_nat[:], ALU.mult, ALU.add)\
                .then_inc(edge_nat_done, 1)
            dve.wait_ge(consts, 6)
            for j in range(EH):
                dve.tensor_reduce(span[:, 0, j:j + 1], dst_nat[:, j, :], AX.X, ALU.min)
                last = dve.tensor_reduce(span[:, 1, j:j + 1], dst_nat[:, j, :], AX.X, ALU.max)
            chain(last)
            for j in range(EH):
                last = dve.tensor_scalar(touch_a[:, j, :], win_lo[:, j, :], span[:, 1, j:j + 1], None, ALU.is_le)
            chain(last)
            for j in range(EH):
                dve.tensor_scalar(touch[:, j, :], win_lo[:, j, :], float(WD), span[:, 0, j:j + 1],
                                  ALU.add, ALU.is_gt).then_inc(vec, 1)
                n[0] += 1
            dve.wait_ge(vec, n[0])
            chain(dve.tensor_tensor(touch[:], touch[:], touch_a[:], ALU.mult))
            for k in range(2):
                for j in range(EH):
                    dve.tensor_scalar(reach[:, k, j, :], touch[:, j, :], tile_id[:, k, j:j + 1], None, ALU.mult)\
                        .then_inc(reach_done, 1)
            dve.wait_ge(edge_t_done, 1)
            dve.tensor_copy(edge_col[:], bank[0][0:EP, 0:2 * ET].rearrange("p (a t) -> p a t", a=2)).then_inc(edge_col_done, 1)
            dve.wait_ge(reach_t_done, 1)
            dve.tensor_reduce(reach_col[:], bank[1][0:2 * EH * NW, 0:EQ], AX.X, ALU.max).then_inc(reach_col_done, 1)
            dve.wait_ge(reach_row_ps, 1)
            chain(dve.tensor_copy(reach_row[:], bank[4][0:1, 0:2 * EH * NW]
                                  .rearrange("p (k j w) -> p k j w", k=2, j=EH)))
            first, end, shift, count = (range_row[:, i, :] for i in range(4))
            chain(dve.tensor_tensor(end, reach_row[:, 0, 0, :], reach_row[:, 0, 1, :], ALU.max))
            chain(dve.tensor_tensor(first, reach_row[:, 1, 0, :], reach_row[:, 1, 1, :], ALU.max))
            chain(dve.tensor_scalar(first, first, -1.0, float(ET), ALU.mult, ALU.add))
            chain(dve.tensor_scalar(first, first, float(ET - 1), None, ALU.min))
            chain(dve.scalar_tensor_tensor(end, first, 1.0, end, ALU.add, ALU.max))
            chain(dve.tensor_tensor(count, end, first, ALU.subtract))
            dve.wait_ge(consts, 8)
            chain(dve.tensor_tensor_scan(shift, count, zero_row[:], 0.0, ALU.add, ALU.add))
            chain(dve.tensor_tensor(shift, shift, end, ALU.subtract))
            chain(dve.tensor_scalar(shift, shift, float(SHIFT), None, ALU.add))
            dve.tensor_copy(range_i[:], range_row[:, 0:3, :]).then_inc(ranges_ready, 1)

            dve.wait_ge(x_in, 32)
            layer_norm_stats(lambda t: x_sb[:, t, :], 1)
            for t in range(NT):
                dve.tensor_scalar(xn[:, t, :], x_sb[:, t, :], mv[:, t, 0:1], rstd[:, t:t + 1],
                                  ALU.subtract, ALU.mult).then_inc(xn_ready, 1)

            def ht_lower(i):
                h, c = Z_OUT[i % 4]
                a, b = HALVES[h]
                dve.wait_ge(ht_hi_done, i + 1)
                dve.tensor_tensor(ht_lo[:, c, a:b], ht_f[:, c, a:b], ht_hi[:, c, a:b].bitcast(f32),
                                  ALU.subtract).then_inc(ht_ready, 1)

            def ys_lower(l, t):
                k = l * NT + t
                dve.wait_ge(ys_hi_done, k + 1)
                dve.tensor_tensor(ys_lo[:, t, :], bank[ys_bank(l, t)][:, :], ys_hi[:, t, :].bitcast(f32),
                                  ALU.subtract).then_inc(ys_ready, 1)

            for i, (h, c) in enumerate(Z_OUT):
                dve.wait_ge(xn_t_done, i + 1)
                a, b = HALVES[h]
                dve.tensor_copy(ht_f[:, c, a:b], bank[i][:, 0:b - a]).then_inc(ht_f_done, 1)
            for i in range(4):
                ht_lower(i)

            def degree(g):
                cols = slice(g * P, (g + 1) * P)
                dve.wait_ge(cnt_done, g + 1)
                dve.tensor_scalar(deg[:], cnt_ps[:, cols], 1.0, None, ALU.max).then_inc(vec, 1)
                dve.tensor_tensor(dg_f[:], cnt_ps[:, cols], ident[:], ALU.mult).then_inc(vec, 1)
                n[0] += 2
                dve.wait_ge(vec, n[0])
                dve.reciprocal(rdeg[:, cols], deg[:]).then_inc(vec, 1)
                n[0] += 1
                chain(dve.tensor_copy(dg_hi[:, g, :], dg_f[:]))
                chain(dve.tensor_tensor(dg_lo[:, g, :], dg_f[:], dg_hi[:, g, :].bitcast(f32), ALU.subtract))
                dve.sem_inc(dg_done, 1)

            dve.wait_ge(ranges_ready, 1)
            dve.wait_ge(edge_col_done, 1)
            for g in range(GROUPS):
                with dve.Fori(g * WPG, (g + 1) * WPG) as w:
                    first_t, end_t, shift_t = load_range(dve, w)
                    with dve.Fori(first_t, end_t) as t:
                        pair = dve.snap(shift_t + t)
                        place = dve.snap(pair & (RING - 1))
                        dve.wait_ge(pair_free, pair)
                        dve.tensor_scalar(hot_lo[:, ds(place, 1), :], iota_lo[0:EP, :], edge_col[:, 0, ds(t, 1)],
                                          None, ALU.is_equal)
                        dve.tensor_scalar(hot_key[:, ds(place, 1), :, :], iota_key[0:EP, :, ds(w * WD, WD)],
                                          edge_col[:, 1, ds(t, 1)], None, ALU.is_equal).then_inc(pair_ready, 1)
                ys_lower(0, g)
                if g:
                    degree(g - 1)
            degree(GROUPS - 1)

            for l in range(LEVELS):
                if l:
                    for t in range(NT):
                        ys_lower(l, t)
                for i, (h, c) in enumerate(Z_OUT):
                    a, b = HALVES[h]
                    dve.wait_ge(z_done, 4 * l + i + 1)
                    dve.scalar_tensor_tensor(ht_f[:, c, a:b], bank[i][:, 0:b - a], 0.0, rdeg[:, a:b],
                                             ALU.max, ALU.mult).then_inc(ht_f_done, 1)
                    ht_lower(4 * (l + 1) + i)

            dve.wait_ge(g_done, 1)
            for t in range(NT):
                dve.tensor_tensor(x1_sb[:, t, :], g_tile(t), x_sb[:, t, :], ALU.add).then_inc(x1_ready, 1)
            dve.wait_ge(x1_ready, NT)
            layer_norm_stats(lambda t: x1_sb[:, t, :], 2)
            for t in range(NT):
                dve.tensor_scalar(x2[:, t, :], x1_sb[:, t, :], mv[:, t, 0:1], rstd[:, t:t + 1],
                                  ALU.subtract, ALU.mult).then_inc(x2_ready, 1)
            dve.wait_ge(x2_ready, NT)
            chain(dve.tensor_copy(x2_hi[:], x2[:]))
            chain(dve.tensor_tensor(x2_lo[:], x2[:], x2_hi[:].bitcast(f32), ALU.subtract))
            for i in range(NT):
                dve.wait_ge(x2_t_ps, i + 1)
                dve.tensor_copy(x2_t[:, :, i * P:(i + 1) * P],
                                bank[i % 2][:, 0:D].rearrange("p (k s) -> p k s", k=KC)).then_inc(x2_t_ready, 1)
            dve.wait_ge(score_ps, 1)
            chain(dve.tensor_copy(score[:], bank[4][:, 0:NT * EXPERTS].rearrange("p (t e) -> p t e", t=NT)))
            for t in range(NT):
                last = dve.max(best[:, t, :], score[:, t, :])
            chain(last)
            for t in range(NT):
                last = dve.max_index(best_id[:, t, :], best[:, t, :], score[:, t, :])
            chain(last)
            chain(dve.tensor_copy(best_f[:], best_id[:, :, 0:2]))
            dve.wait_ge(ffn_consts, 5)
            chain(dve.tensor_scalar(valid[:], node_id[:], float(NODES), None, ALU.is_lt))
            for k in range(2):
                last = dve.tensor_tensor(pick[:, k, :, :], iota_e[:], best_f[:, :, k:k + 1].broadcast_to((P, NT, EXPERTS)),
                                         ALU.is_equal)
            chain(last)
            chain(dve.tensor_tensor(both[:], pick[:, 0, :, :], pick[:, 1, :, :], ALU.add))
            chain(dve.tensor_tensor(both[:], both[:], valid[:].unsqueeze(2).broadcast_to((P, NT, EXPERTS)), ALU.mult))
            dve.tensor_copy(both_bf[:], both[:]).then_inc(both_ready, 1)
            dve.wait_ge(prefix_ps, 1)
            sums = bank[4][:, 128:128 + NT * EXPERTS].rearrange("p (t e) -> p t e", t=NT)
            before = bank[4][:, 256:256 + NT * EXPERTS].rearrange("p (t e) -> p t e", t=NT)
            chain(dve.tensor_copy(tile_sum[:, 0, :], zeros_e[:]))
            for t in range(NT):
                chain(dve.tensor_tensor(tile_sum[:, t + 1, :], tile_sum[:, t, :], sums[:, t, :], ALU.add))
            chain(dve.tensor_scalar(tiles_i[:, 0, :], tile_sum[:, NT, :], float(P - 1), None, ALU.add))
            chain(dve.tensor_single_scalar(tiles_i[:, 1, :], tiles_i[:, 0, :], 7, ALU.arith_shift_right))
            chain(dve.tensor_copy(tiles_f[:], tiles_i[:, 1, :]))
            chain(dve.tensor_tensor_scan(tiles_end[:], tiles_f[:], zeros_e[:], 0.0, ALU.add, ALU.add))
            chain(dve.tensor_tensor(slot0[:], tiles_end[:], tiles_f[:], ALU.subtract))
            chain(dve.tensor_scalar(slot0[:], slot0[:], float(P), None, ALU.mult))
            chain(dve.tensor_tensor(slot[:], before, tile_sum[:, 0:NT, :], ALU.add))
            chain(dve.tensor_tensor(slot[:], slot[:], slot0[:].unsqueeze(1).broadcast_to((P, NT, EXPERTS)), ALU.add))
            chain(dve.scalar_tensor_tensor(slot_hot[:], slot[:].rearrange("p t e -> p e t"), 1.0,
                                           both[:].rearrange("p t e -> p e t"), ALU.add, ALU.mult))
            chain(dve.tensor_scalar(slot_hot[:], slot_hot[:], 1.0, None, ALU.subtract))
            chain(dve.tensor_tensor(past[:], iota_s[:], tiles_end[0:1, :].unsqueeze(1)
                                    .broadcast_to((1, SLOT_TILES, EXPERTS)), ALU.is_ge))
            chain(dve.tensor_reduce(owner[:, 0:SLOT_TILES], past[:], AX.X, ALU.add))
            chain(dve.tensor_scalar(owner[:, 0:SLOT_TILES], owner[:, 0:SLOT_TILES], float(EXPERTS - 1), None, ALU.min))
            chain(dve.tensor_copy(owner[:, SLOT_TILES:], tiles_end[0:1, EXPERTS - 1:EXPERTS]))
            dve.tensor_copy(owner_i[:], owner[:]).then_inc(route_ready, 1)

            def expert_of(s):
                return dve.value_load(owner_i[0:1, ds(s, 1)], min_val=0, max_val=EXPERTS - 1)

            def one_hot(s):
                e = expert_of(s)
                for t in range(NT):
                    last = dve.tensor_scalar(hot_slot[:, t, :], iota_slot[:, ds(s, 1), :], slot_hot[:, ds(e, 1), t],
                                             None, ALU.is_equal)
                last.then_inc(hot_ready, 1)

            def add_b1(s):
                e = expert_of(s)
                dve.tensor_tensor(h_pre[:], bank[1][:, :], b1_bc[:, ds(e, 1), :], ALU.add).then_inc(pre_ready, 1)

            dve.wait_ge(route_ready, 1)
            one_hot(0)
            dve.wait_ge(gathered, 1)
            one_hot(1)
            for k in range(2):
                last = dve.tensor_tensor(slot_pick[:, k, :, :], pick[:, k, :, :], slot[:], ALU.mult)
            chain(last)
            chain(dve.tensor_reduce(slot_of[:], slot_pick[:], AX.X, ALU.add))
            chain(dve.tensor_copy(slot_idx[:], slot_of[:]))
            dve.sem_inc(route_ready, 1)
            dve.wait_ge(ffn_b_in, 16 * (EXPERTS + 1))
            dve.wait_ge(up_done, 1)
            add_b1(0)
            dve.wait_ge(gathered, 2)
            one_hot(2)
            tiles = dve.value_load(owner_i[0:1, SLOT_TILES:SLOT_TILES + 1], min_val=MIN_TILES, max_val=MAX_TILES)
            with dve.Fori(0, tiles) as s:
                dve.wait_ge(t_done, s + 1)
                dve.tensor_copy(h_t[:], bank[2].rearrange("p (k s) -> p k s", k=HC)).then_inc(h_t_ready, 1)
                dve.wait_ge(up_done, s + 2)
                dve.wait_ge(act_ready, s + 1)
                add_b1(s + 1)
                dve.wait_ge(gathered, s + 3)
                one_hot(s + 3)
                e = expert_of(s)
                dve.wait_ge(down_done, s + 1)
                dve.tensor_tensor(y_sb[:, ds(s, 1), :], bank[3][:, 0:D], b2_bc[:, ds(e, 1), :], ALU.add)\
                    .then_inc(y_ready, 1)
            for t in range(NT):
                dve.wait_ge(y_in[t], 32)
                rows = P if t < NT - 1 else LAST
                chain(dve.tensor_tensor(x1_sb[0:rows, t, :], x1_sb[0:rows, t, :], y_back[0:rows, t, 0, :], ALU.add))
                dve.tensor_tensor(x1_sb[0:rows, t, :], x1_sb[0:rows, t, :], y_back[0:rows, t, 1, :], ALU.add)\
                    .then_inc(out_ready, 1)

        @block.tensor
        def _(pe):
            def exact3(out_, lhs, rhs, first, last):
                (lh, ll), (rh, rl) = lhs, rhs
                pe.matmul(out_, lh, rh, start=first, stop=False, skip_group_check=True)
                pe.matmul(out_, lh, rl, start=False, stop=False, skip_group_check=True)
                return pe.matmul(out_, ll, rh, start=False, stop=last, skip_group_check=True)

            pe.wait_ge(consts, 1)
            pe.wait_ge(edge_nat_done, 2)
            for a in range(2):
                for j in range(EH):
                    o = a * ET + j * EQ
                    last = pe.transpose(bank[0][0:EP, o:o + EQ], edge_nat[:, a, j, :], ident[0:EQ, 0:EQ])
            last.then_inc(edge_t_done, 1)
            pe.wait_ge(reach_done, 2 * EH)
            pe.transpose(bank[1][0:2 * EH * NW, 0:EQ], reach[:].rearrange("q k j w -> q (k j w)"),
                         ident[0:EQ, 0:EQ]).then_inc(reach_t_done, 1)
            pe.wait_ge(reach_col_done, 1)
            pe.transpose(bank[4][0:1, 0:2 * EH * NW], reach_col[:], ident[0:2 * EH * NW, 0:2 * EH * NW])\
                .then_inc(reach_row_ps, 1)
            pe.wait_ge(edge_t_done, 1)
            for i, (h, c) in enumerate(Z_OUT):
                a, b = HALVES[h]
                if i == 0:
                    pe.wait_ge(edge_col_done, 1)
                for t in range(a // P, b // P):
                    pe.wait_ge(xn_ready, t + 1)
                    last = pe.transpose(bank[i][:, t * P - a:(t + 1) * P - a], xn[:, t, c * P:(c + 1) * P], ident[:])
                last.then_inc(xn_t_done, 1)

            def ys_product(l, t):
                r, cols, o = l % 2, slice(t * P, (t + 1) * P), bank[ys_bank(l, t)]
                for k in range(KC):
                    exact3(o[:, :], (ht_hi[:, k, cols], ht_lo[:, k, cols]),
                           (w_hi[:, r, k, 0:2 * D], w_lo[:, r, k, 0:2 * D]), k == 0, False)
                pe.matmul(o[:, D:2 * D], row_pick[:, l, :], b_hi[:], start=False, stop=False,
                          skip_group_check=True)
                pe.matmul(o[:, D:2 * D], row_pick[:, l, :], b_lo[:], start=False, stop=True,
                          skip_group_check=True).then_inc(ys_done, 1)

            def g_product(l, t):
                r, cols = l % 2, slice(t * P, (t + 1) * P)
                for k in range(KC):
                    last = exact3(g_tile(t), (ht_hi[:, k, cols], ht_lo[:, k, cols]),
                                  (w_hi[:, r, k, 2 * D:], w_lo[:, r, k, 2 * D:]), False,
                                  l == LEVELS and k == KC - 1)
                return last

            pe.wait_ge(b_split, 2)
            for t in range(NT):
                pe.matmul(g_tile(t), row_pick[:, LEVELS, :], b_hi[:], start=t % 2 == 0, stop=False,
                          skip_group_check=True)
                pe.matmul(g_tile(t), row_pick[:, LEVELS, :], b_lo[:], start=False, stop=False,
                          skip_group_check=True)

            pe.wait_ge(consts, 12)
            pe.wait_ge(ranges_ready, 1)
            pe.wait_ge(ht_f_done, 4)
            pe.sem_inc(pair_free, SHIFT + RING - 1)
            pe.sem_inc(pair_ready, SHIFT - 1)
            for g in range(GROUPS):
                with pe.Fori(g * (WPG // 2), (g + 1) * (WPG // 2)) as w2:
                    for half in range(2):
                        w = w2 * 2 + half
                        pane = bank[half][:, 0:NT * WD]
                        first_t, end_t, shift_t = load_range(pe, w)
                        pe.wait_ge(window_free, w + 1)
                        pe.matmul(pane, zeros_bf[:, 0:P], zeros_bf[:], start=True, stop=False, skip_group_check=True)
                        with pe.Fori(first_t, end_t) as t:
                            pair = pe.snap(shift_t + t)
                            place = pe.snap(pair & (RING - 1))
                            pe.wait_ge(pair_ready, pair)
                            pe.matmul(pane, hot_lo[:, ds(place, 1), :].rearrange("p a m -> p (a m)"),
                                      hot_key[:, ds(place, 1), :, :].rearrange("p a n w -> p (a n w)"),
                                      start=False, stop=False, skip_group_check=True).then_inc(pair_free, 1)
                        pe.matmul(pane, zeros_bf[:, 0:P], zeros_bf[:], start=False, stop=True,
                                  skip_group_check=True).then_inc(window_done, 1)
                if g == 0:
                    pe.wait_ge(w_split, 1)
                    pe.wait_ge(ht_ready, 4)
                if g:
                    pe.wait_ge(ys_ready, g)
                ys_product(0, g)
                g_product(0, g)
                cols = slice(g * P, (g + 1) * P)
                pe.wait_ge(a_lo_done, g + 1)
                if g:
                    pe.wait_ge(dg_done, g)
                for u in range(NT):
                    pe.matmul(cnt_ps[:, cols], ones_sq[:], a_hi[:, u, cols], start=u == 0, stop=False,
                              skip_group_check=True)
                    last = pe.matmul(cnt_ps[:, cols], ones_sq[:], a_lo[:, u, cols], start=False,
                                     stop=u == NT - 1, skip_group_check=True)
                last.then_inc(cnt_done, 1)

            for l in range(LEVELS):
                if l:
                    pe.wait_ge(w_split, l + 1)
                    for t in range(NT):
                        pe.wait_ge(ht_ready, 4 * l + (2 if t < 3 else 4))
                        if t >= 2:
                            pe.wait_ge(ys_ready, l * NT + t - 1)
                        ys_product(l, t)
                    for t in range(NT):
                        g_product(l, t)
                if l == 0:
                    pe.wait_ge(dg_done, GROUPS)
                for i, (h, c) in enumerate(Z_OUT):
                    a, b = HALVES[h]
                    o = bank[i]
                    m = slice(c * P, (c + 1) * P)
                    ms = slice(D + c * P, D + (c + 1) * P)
                    for u in range(NT):
                        if i == 0:
                            pe.wait_ge(ys_ready, l * NT + (u + 1 if l == 0 else max(u + 1, NT - 1)))
                        exact3(o[:, 0:b - a], (ys_hi[:, u, m], ys_lo[:, u, m]),
                               (a_hi[:, u, a:b], a_lo[:, u, a:b]), u == 0, False)
                    for j in range(a // P, b // P):
                        last = exact3(o[:, j * P - a:(j + 1) * P - a], (ys_hi[:, j, ms], ys_lo[:, j, ms]),
                                      (dg_hi[:, j, :], dg_lo[:, j, :]), False, j == b // P - 1)
                    last.then_inc(z_done, 1)
            pe.wait_ge(w_split, LEVELS + 1)
            for t in range(NT):
                pe.wait_ge(ht_ready, 4 * LEVELS + (2 if t < 3 else 4))
                last = g_product(LEVELS, t)
            last.then_inc(g_done, 1)

            for t in range(NT):
                pe.wait_ge(x2_ready, t + 1)
                if t >= 2:
                    pe.wait_ge(x2_t_ready, t - 1)
                for k in range(KC):
                    last = pe.transpose(bank[t % 2][:, k * P:(k + 1) * P], x2[:, t, k * P:(k + 1) * P], ident[:])
                last.then_inc(x2_t_ps, 1)
            pe.wait_ge(ffn_w_in, 16 * (2 + 2 * EXPERTS))
            for t in range(NT):
                pe.wait_ge(x2_t_ready, t + 1)
                o = bank[4][:, t * EXPERTS:(t + 1) * EXPERTS]
                for k in range(KC):
                    pe.matmul(o, x2_t[:, k, t * P:(t + 1) * P], wg_sb[:, k, :], start=k == 0, stop=False,
                              skip_group_check=True)
                last = pe.matmul(o, ones_rowf[:], bg_row[:], start=False, stop=True, skip_group_check=True)
            last.then_inc(score_ps, 1)
            pe.wait_ge(both_ready, 1)
            picked = both_bf[:].rearrange("p t e -> p (t e)")
            pe.matmul(bank[4][:, 128:128 + NT * EXPERTS], ones_bf[:], picked, start=True, stop=True)
            pe.matmul(bank[4][:, 256:256 + NT * EXPERTS], tri_bf[:], picked, start=True, stop=True)\
                .then_inc(prefix_ps, 1)

            def gather(s):
                pe.wait_ge(hot_ready, s + 1)
                for k in range(KC):
                    o = bank[0][:, k * P:(k + 1) * P]
                    for t in range(NT):
                        pe.matmul(o, x2_hi[:, t, k * P:(k + 1) * P], hot_slot[:, t, :], start=t == 0, stop=False,
                                  skip_group_check=True)
                        last = pe.matmul(o, x2_lo[:, t, k * P:(k + 1) * P], hot_slot[:, t, :], start=False,
                                         stop=t == NT - 1, skip_group_check=True)
                last.then_inc(gathered, 1)

            def up(s):
                e = pe.value_load(owner_i[0:1, ds(s, 1)], min_val=0, max_val=EXPERTS - 1)
                pe.wait_ge(xt_ready, s + 1)
                for k in range(KC):
                    last = pe.matmul(bank[1][:, :], xt[:, k, :], w1_sb[:, ds(e, 1), k, :], start=k == 0,
                                     stop=k == KC - 1)
                last.then_inc(up_done, 1)

            pe.wait_ge(route_ready, 1)
            gather(0)
            pe.wait_ge(xt_ready, 1)
            gather(1)
            up(0)
            tiles = pe.value_load(owner_i[0:1, SLOT_TILES:SLOT_TILES + 1], min_val=MIN_TILES, max_val=MAX_TILES)
            with pe.Fori(0, tiles) as s:
                pe.wait_ge(act_ready, s + 1)
                for k in range(HC):
                    last = pe.transpose(bank[2][:, k * P:(k + 1) * P], h_act[:, k * P:(k + 1) * P], ident[:])
                last.then_inc(t_done, 1)
                up(s + 1)
                e = pe.value_load(owner_i[0:1, ds(s, 1)], min_val=0, max_val=EXPERTS - 1)
                pe.wait_ge(h_t_ready, s + 1)
                for k in range(HC):
                    last = pe.matmul(bank[3][:, 0:D], h_t[:, k, :], w2_sb[:, ds(e, 1), k, :], start=k == 0,
                                     stop=k == HC - 1)
                last.then_inc(down_done, 1)
                gather(s + 2)


_INS = ["x", "src", "dst"] + [f"L0_gnn_{n}" for n in ("W0", "b0", "W1", "b1", "W2", "b2", "Wf", "bf")] \
    + [f"L0_ffn_{n}" for n in ("Wg", "bg", "W1", "b1", "W2", "b2")]


def kernel(**inputs):
    import concourse.bacc as bacc
    from concourse.bass_utils import run_bass_kernel_spmd

    nc = bacc.Bacc("TRN2", target_bir_lowering=False, num_devices=1)
    arrays, ap = {}, {}
    for name in _INS:
        a = np.ascontiguousarray(inputs[name])
        arrays[f"in_{name}"] = a
        ap[name] = nc.dram_tensor(f"in_{name}", a.shape, mybir.dt.from_np(a.dtype), kind="ExternalInput").ap()
    out = nc.dram_tensor("out_rows", (NODES, D), mybir.dt.float32, kind="ExternalOutput").ap()
    g = {n: ap[f"L0_gnn_{n}"] for n in ("W0", "b0", "W1", "b1", "W2", "b2", "Wf", "bf")}
    f = {n: ap[f"L0_ffn_{n}"] for n in ("Wg", "bg", "W1", "b1", "W2", "b2")}
    build(nc, ap["x"], ap["src"], ap["dst"], [g["W0"], g["W1"], g["W2"]], [g["b0"], g["b1"], g["b2"]],
          g["Wf"], g["bf"], f["Wg"], f["bg"], f["W1"], f["b1"], f["W2"], f["b2"], out)
    r = run_bass_kernel_spmd(nc, [arrays], core_ids=[0])
    return r.results[0]["out_rows"]
```

```python
import concourse.bass as bass
from concourse import mybir
from contextlib import ExitStack
import numpy as np

NODES = 625
EDGES = 20000
D = 256
LEVELS = 3
EXPERTS = 8
HID = 512
EPS = 1e-5

P = 128
NT = -(-NODES // P)
NPAD = NT * P
LAST = NODES - (NT - 1) * P
KC = D // P
HC = HID // P

EP = 125
ET = EDGES // EP
EH = 2
EQ = ET // EH
assert EP * ET == EDGES and EQ * EH == ET and EQ <= P

CT = 5
CHUNKS = ET // CT
UNROLL = 4
TURNS = CHUNKS // UNROLL
WD = 48
AW = NPAD + WD
MAX_PASSES = -(-NODES // WD)
KEY = 1024
EXACT = 4096
COVER = EXACT // (CT * EP)
SEGMENTS = 4

MAX_TILES = (2 * NODES + EXPERTS * (P - 1)) // P
MIN_TILES = -(-2 * NODES // P)
AHEAD = 3
SLOT_TILES = MAX_TILES + AHEAD


def build(nc, x, src, dst, W, B, Wf, bf, Wg, bg, W1, b1, W2, b2, out):
    f32, f32r = mybir.dt.float32, mybir.dt.float32r
    bf16, i32, i16, u32 = mybir.dt.bfloat16, mybir.dt.int32, mybir.dt.int16, mybir.dt.uint32
    ALU = mybir.AluOpType
    ACT = mybir.ActivationFunctionType
    AX = mybir.AxisListType
    ds = bass.ds

    ys_dram = nc.dram_tensor("ys_rows", [MAX_TILES * P, D], f32, kind="Internal").ap()

    ctx = ExitStack()
    with ctx:
        def sb(name, shape, dt, scope=ctx):
            return scope.enter_context(nc.sbuf_tensor(name, shape, dt))

        def sem(name):
            return ctx.enter_context(nc.semaphore(name))

        w1_sb = sb("w1_sb", [P, EXPERTS, KC, HID], f32)
        w2_sb = sb("w2_sb", [P, EXPERTS, HC, D], f32)
        wg_sb = sb("wg_sb", [P, KC, EXPERTS], f32)
        bg_row = sb("bg_row", [1, EXPERTS], f32)
        x_sb = sb("x_sb", [P, NT, D], f32)
        x1_sb = sb("x1_sb", [P, NT, D], f32)
        ident = sb("ident", [P, P], f32)
        ones_rowf = sb("ones_rowf", [1, P], f32)
        ones_sq = sb("ones_sq", [P, P], f32r)
        ones_bf = sb("ones_bf", [P, P], bf16)
        tri_bf = sb("tri_bf", [P, P], bf16)
        stats = sb("stats", [P, NT, 6], f32)
        mv = sb("mv", [P, NT, 2], f32)
        std = sb("std", [P, NT], f32)
        rstd = sb("rstd", [P, NT], f32)
        var_eps = sb("var_eps", [P, NT], f32)
        newton = sb("newton", [P, NT], f32)
        iota_lo = sb("iota_lo", [P, P], i16)

        gnn = ExitStack()
        w_stage = sb("w_stage", [P, 3, KC, D], f32, gnn)
        w_hi = sb("w_hi", [P, 2, KC, 3 * D], f32r, gnn)
        w_lo = sb("w_lo", [P, 2, KC, 3 * D], f32r, gnn)
        b_rows = sb("b_rows", [LEVELS + 1, D], f32, gnn)
        b_hi = sb("b_hi", [LEVELS + 1, D], f32r, gnn)
        b_lo = sb("b_lo", [LEVELS + 1, D], f32r, gnn)
        row_pick = sb("row_pick", [LEVELS + 1, LEVELS + 1, P], f32r, gnn)
        a_f = sb("a_f", [P, NT, AW], f32, gnn)
        a_hi = sb("a_hi", [P, NT, AW], f32r, gnn)
        rdeg = sb("rdeg", [P, NPAD], f32, gnn)
        dg_f = sb("dg_f", [P, NT, P], f32, gnn)
        dg_hi = sb("dg_hi", [P, NT, P], f32r, gnn)
        ht_f = sb("ht_f", [P, KC, NPAD], f32, gnn)
        ht_hi = sb("ht_hi", [P, KC, NPAD], f32r, gnn)
        ht_lo = sb("ht_lo", [P, KC, NPAD], f32r, gnn)
        ys_hi = sb("ys_hi", [P, NT, 2 * D], f32r, gnn)
        ys_lo = sb("ys_lo", [P, NT, 2 * D], f32r, gnn)
        xn = x1_sb
        src_nat = sb("src_nat", [EQ, EH, EP], i32, gnn)
        dst_nat = sb("dst_nat", [EQ, EH, EP], i32, gnn)
        dst_chunk = sb("dst_chunk", [CHUNKS, CT * EP], i32, gnn)
        hi_nat = sb("hi_nat", [EQ, EH, EP], i32, gnn)
        lo_nat = sb("lo_nat", [EQ, EH, EP], i32, gnn)
        edge_nat = sb("edge_nat", [EQ, 2, EH, EP], f32, gnn)
        edge_key = sb("edge_key", [EP, ET], f32, gnn)
        edge_rel = sb("edge_rel", [EP, 2, ET], f32, gnn)
        edge_turn = sb("edge_turn", [EP, 2, UNROLL * CT], f32, gnn)
        span = sb("span", [CHUNKS, 2], f32, gnn)
        span_diag = sb("span_diag", [CHUNKS, 2, CHUNKS], f32, gnn)
        span_bc = sb("span_bc", [P, 2, CHUNKS], f32, gnn)
        width = sb("width", [1, CHUNKS], f32, gnn)
        widest = sb("widest", [1, 1], f32, gnn)
        steps = sb("steps", [1, MAX_PASSES], f32, gnn)
        needed = sb("needed", [1, MAX_PASSES], f32, gnn)
        covers = sb("covers", [CHUNKS, CHUNKS], f32, gnn)
        cover_row = sb("cover_row", [1, 2], f32, gnn)
        meta = sb("meta", [1, 2], f32, gnn)
        meta_i = sb("meta_i", [1, 2], i32, gnn)
        base_i = sb("base_i", [1, CHUNKS], i32, gnn)
        iota_key = sb("iota_key", [P, NT, WD], i16, gnn)
        hot_lo = sb("hot_lo", [EP, UNROLL * CT, P], bf16, gnn)
        hot_key = sb("hot_key", [EP, UNROLL * CT, NT, WD], bf16, gnn)
        gnn.close()

        ffn = ExitStack()
        b1_bc = sb("b1_bc", [P, EXPERTS, HID], f32, ffn)
        b2_bc = sb("b2_bc", [P, EXPERTS, D], f32, ffn)
        x2 = sb("x2", [P, NT, D], f32, ffn)
        x2_hi = sb("x2_hi", [P, NT, D], f32r, ffn)
        x2_lo = sb("x2_lo", [P, NT, D], f32r, ffn)
        x2_t = sb("x2_t", [P, KC, NPAD], f32, ffn)
        score = sb("score", [P, NT, EXPERTS], f32, ffn)
        best = sb("best", [P, NT, 8], f32, ffn)
        best_id = sb("best_id", [P, NT, 8], u32, ffn)
        best_f = sb("best_f", [P, NT, 2], f32, ffn)
        iota_e = sb("iota_e", [P, NT, EXPERTS], f32, ffn)
        node_id = sb("node_id", [P, NT], f32, ffn)
        valid = sb("valid", [P, NT], f32, ffn)
        pick = sb("pick", [P, 2, NT, EXPERTS], f32, ffn)
        both = sb("both", [P, NT, EXPERTS], f32, ffn)
        both_bf = sb("both_bf", [P, NT, EXPERTS], bf16, ffn)
        tile_sum = sb("tile_sum", [P, NT + 1, EXPERTS], f32, ffn)
        tiles_i = sb("tiles_i", [P, 2, EXPERTS], i32, ffn)
        tiles_f = sb("tiles_f", [P, EXPERTS], f32, ffn)
        tiles_end = sb("tiles_end", [P, EXPERTS], f32, ffn)
        zeros_e = sb("zeros_e", [P, EXPERTS], f32, ffn)
        slot0 = sb("slot0", [P, EXPERTS], f32, ffn)
        slot = sb("slot", [P, NT, EXPERTS], f32, ffn)
        slot_hot = sb("slot_hot", [P, EXPERTS, NT], f32, ffn)
        slot_pick = sb("slot_pick", [P, 2, NT, EXPERTS], f32, ffn)
        slot_of = sb("slot_of", [P, 2, NT], f32, ffn)
        slot_idx = sb("slot_idx", [P, 2, NT], u32, ffn)
        iota_s = sb("iota_s", [1, SLOT_TILES, EXPERTS], f32, ffn)
        past = sb("past", [1, SLOT_TILES, EXPERTS], f32, ffn)
        owner = sb("owner", [1, SLOT_TILES + 1], f32, ffn)
        owner_i = sb("owner_i", [1, SLOT_TILES + 1], i32, ffn)
        iota_slot = sb("iota_slot", [P, SLOT_TILES, P], i16, ffn)
        hot_slot = sb("hot_slot", [P, NT, P], f32r, ffn)
        xt = sb("xt", [P, KC, P], f32, ffn)
        h_pre = sb("h_pre", [P, HID], f32, ffn)
        h_act = sb("h_act", [P, HID], f32, ffn)
        h_t = sb("h_t", [P, HC, P], f32, ffn)
        y_sb = sb("y_sb", [P, SLOT_TILES, D], f32, ffn)
        y_back = sb("y_back", [P, NT, 2, D], f32, ffn)
        ffn.close()

        bank = [ctx.enter_context(nc.psum_tensor(f"bank{i}", [P, 512], f32)) for i in range(2)]
        cnt_ps = ctx.enter_context(nc.psum_tensor("cnt_ps", [P, 1024], f32))
        bank += [cnt_ps[:, 0:512], cnt_ps[:, 512:1024]]
        bank += [ctx.enter_context(nc.psum_tensor("bank4", [P, 512], f32))]
        g_ps = [ctx.enter_context(nc.psum_tensor(f"g_ps{i}", [P, 512], f32)) for i in range(3)]

        def g_tile(t):
            return g_ps[t // 2][:, (t % 2) * D:(t % 2) * D + D]

        edges_in = sem("edges_in")
        chunks_in = sem("chunks_in")
        x_in = sem("x_in")
        small_in = sem("small_in")
        w_in = [sem(f"w_in{l}") for l in range(LEVELS + 1)]
        ffn_w_in = sem("ffn_w_in")
        ffn_b_in = sem("ffn_b_in")
        consts = sem("consts")
        x_zeroed = sem("x_zeroed")
        pool_chain = sem("pool_chain")
        w_split = sem("w_split")
        b_split = sem("b_split")
        ffn_consts = sem("ffn_consts")
        vec = sem("vec")
        edge_nat_done = sem("edge_nat_done")
        span_ready = sem("span_ready")
        span_ps = sem("span_ps")
        covers_ready = sem("covers_ready")
        covers_ps = sem("covers_ps")
        edge_t_done = sem("edge_t_done")
        edge_col_done = sem("edge_col_done")
        base_ready = sem("base_ready")
        a_zeroed = sem("a_zeroed")
        window_moved = sem("window_moved")
        pass_begun = sem("pass_begun")
        var_ready = sem("var_ready")
        std_ready = sem("std_ready")
        xn_ready = sem("xn_ready")
        xn_t_done = sem("xn_t_done")
        ht_hi_done = sem("ht_hi_done")
        ht_f_done = sem("ht_f_done")
        ht_ready = sem("ht_ready")
        turn_ready = sem("turn_ready")
        hot_chunk = sem("hot_chunk")
        chunk_free = sem("chunk_free")
        chunk_done = sem("chunk_done")
        a_written = sem("a_written")
        pane_free = sem("pane_free")
        a_complete = sem("a_complete")
        cnt_done = sem("cnt_done")
        dg_done = sem("dg_done")
        ys_done = sem("ys_done")
        ys_hi_done = sem("ys_hi_done")
        ys_ready = sem("ys_ready")
        z_done = sem("z_done")
        g_done = sem("g_done")
        x1_ready = sem("x1_ready")
        x2_ready = sem("x2_ready")
        x2_t_ps = sem("x2_t_ps")
        x2_t_ready = sem("x2_t_ready")
        score_ps = sem("score_ps")
        both_ready = sem("both_ready")
        prefix_ps = sem("prefix_ps")
        route_ready = sem("route_ready")
        hot_ready = sem("hot_ready")
        gathered = sem("gathered")
        xt_ready = sem("xt_ready")
        up_done = sem("up_done")
        pre_ready = sem("pre_ready")
        act_ready = sem("act_ready")
        t_done = sem("t_done")
        h_t_ready = sem("h_t_ready")
        down_done = sem("down_done")
        y_ready = sem("y_ready")
        y_stored = sem("y_stored")
        rows_filled = sem("rows_filled")
        rows_stored = sem("rows_stored")
        y_in = [sem(f"y_in{t}") for t in range(NT)]
        out_ready = sem("out_ready")
        out_stored = sem("out_stored")

        block = ctx.enter_context(nc.Block())

        x_rows = x[0:(NT - 1) * P, :].rearrange("(t p) d -> p t d", p=P)
        HALVES = [(0, 3 * P), (3 * P, NPAD)]
        Z_OUT = [(h, c) for h in range(2) for c in range(KC)]

        def ys_bank(l, t):
            return (4, 2, 3)[t % 3] if l == 0 else (4, 0)[t % 2]

        SEG_TILES = [[0, 1], [2, 3], [4], []]

        def gather_ps():
            return bank[0][:, 0:D].rearrange("p (k s) -> p k s", k=KC)

        def passes(eng):
            return eng.value_load(meta_i[0:1, 0:1], min_val=1, max_val=MAX_PASSES)

        def window_start(eng, c):
            return eng.value_load(base_i[0:1, ds(c, 1)], min_val=0, max_val=NPAD)

        @block.sync
        def _(sp):
            sp.dma_start(dst_nat[:], dst.rearrange("(j q e) -> q j e", j=EH, e=EP)).then_inc(edges_in, 16)
            sp.dma_start(src_nat[:], src.rearrange("(j q e) -> q j e", j=EH, e=EP)).then_inc(edges_in, 16)
            sp.dma_start(dst_chunk[:], dst.rearrange("(c e) -> c e", c=CHUNKS)).then_inc(chunks_in, 16)
            sp.wait_ge(x_zeroed, 1)
            sp.dma_start(x_sb[:, 0:NT - 1, :], x_rows).then_inc(x_in, 16)
            sp.dma_start(x_sb[0:LAST, NT - 1, :], x[(NT - 1) * P:NODES, :]).then_inc(x_in, 16)
            for i, b in enumerate(B + [bf]):
                sp.dma_start(b_rows[i:i + 1, :], b.unsqueeze(0)).then_inc(small_in, 16)
            for l in range(LEVELS + 1):
                if l:
                    sp.wait_ge(w_split, l)
                if l < LEVELS:
                    sp.dma_start(w_stage[:, 0:2, :, :],
                                 W[l].rearrange("(h k p) d -> p h k d", h=2, k=KC)).then_inc(w_in[l], 16)
                sp.dma_start(w_stage[:, 2, :, :],
                             Wf[l * D:(l + 1) * D, :].rearrange("(k p) d -> p k d", k=KC)).then_inc(w_in[l], 16)
            sp.dma_start(wg_sb[:], Wg.rearrange("(k p) e -> p k e", k=KC)).then_inc(ffn_w_in, 16)
            sp.dma_start(bg_row[:], bg.unsqueeze(0)).then_inc(ffn_w_in, 16)
            for e in range(EXPERTS):
                sp.dma_start(w1_sb[:, e, :, :], W1[e].rearrange("(k p) h -> p k h", k=KC)).then_inc(ffn_w_in, 16)
                sp.dma_start(w2_sb[:, e, :, :], W2[e].rearrange("(k p) d -> p k d", k=HC)).then_inc(ffn_w_in, 16)
            sp.dma_start(ys_dram[MIN_TILES * P:, :],
                         W1.rearrange("e k (a d) -> (e k a) d", d=D)[0:(MAX_TILES - MIN_TILES) * P, :])\
                .then_inc(rows_filled, 16)
            sp.wait_ge(x1_ready, NT)
            for e in range(EXPERTS):
                sp.dma_start(b1_bc[:, e, :], b1[e].partition_broadcast(P)).then_inc(ffn_b_in, 16)
            sp.dma_start(b2_bc[:], b2.rearrange("e d -> (e d)").partition_broadcast(P)
                         .rearrange("p (e d) -> p e d", e=EXPERTS)).then_inc(ffn_b_in, 16)
            sp.wait_ge(route_ready, 1)
            tiles = sp.value_load(owner_i[0:1, SLOT_TILES:SLOT_TILES + 1], min_val=MIN_TILES, max_val=MAX_TILES)
            sp.wait_ge(rows_filled, 16)
            with sp.Fori(0, tiles) as s:
                sp.wait_ge(y_ready, s + 1)
                sp.dma_start(ys_dram[ds(s * P, P), :], y_sb[:, ds(s, 1), :]).then_inc(y_stored, 16)
            for t in range(NT):
                rows = P if t < NT - 1 else LAST
                sp.wait_ge(out_ready, t + 1)
                sp.dma_start(out[t * P:t * P + rows, :], x1_sb[0:rows, t, :]).then_inc(out_stored, 16)
            sp.wait_ge(out_stored, 16 * NT)

        @block.gpsimd
        def _(pool):
            n = [0]

            def chain(ins):
                n[0] += 1
                ins.then_inc(pool_chain, 1)
                pool.wait_ge(pool_chain, n[0])

            pool.memset(x_sb[:, NT - 1, :], 0.0).then_inc(x_zeroed, 1)
            chain(pool.memset(ident[:], 0.0))
            pool.affine_select(out=ident[:], in_=ident[:], compare_op=ALU.not_equal, fill=1.0, base=0,
                               pattern=[[-1, P]], channel_multiplier=1).then_inc(consts, 1)
            pool.iota(iota_lo[:], pattern=[[1, P]], base=0, channel_multiplier=0,
                      allow_small_or_imprecise_dtypes=True).then_inc(consts, 1)
            pool.iota(iota_key[:], pattern=[[KEY, NT], [1, WD]], base=0, channel_multiplier=0,
                      allow_small_or_imprecise_dtypes=True).then_inc(consts, 1)
            pool.iota(steps[:], pattern=[[WD, MAX_PASSES]], base=0, channel_multiplier=0,
                      allow_small_or_imprecise_dtypes=True).then_inc(consts, 1)
            pool.memset(ones_rowf[:], 1.0).then_inc(consts, 1)
            pool.memset(ones_sq[:].bitcast(f32), 1.0).then_inc(consts, 1)
            pool.memset(ones_bf[:], 1.0).then_inc(consts, 1)
            chain(pool.memset(tri_bf[:], 0.0))
            pool.affine_select(out=tri_bf[:], in_=tri_bf[:], compare_op=ALU.is_ge, fill=1.0, base=0,
                               pattern=[[-1, P]], channel_multiplier=1).then_inc(consts, 1)
            pool.memset(a_f[:], 0.0).then_inc(a_zeroed, 1)
            pool.memset(a_hi[:].bitcast(f32), 0.0).then_inc(a_zeroed, 1)
            pool.wait_ge(consts, 1)
            pool.tensor_copy(row_pick[:], ident[0:LEVELS + 1, 0:LEVELS + 1].unsqueeze(2)
                             .broadcast_to((LEVELS + 1, LEVELS + 1, P))).then_inc(b_split, 1)
            pool.wait_ge(small_in, 16 * (LEVELS + 1))
            chain(pool.tensor_copy(b_hi[:], b_rows[:]))
            pool.tensor_tensor(b_lo[:], b_rows[:], b_hi[:].bitcast(f32), ALU.subtract).then_inc(b_split, 1)

            def split_weights(l):
                r = l % 2
                pool.wait_ge(w_in[l], 32 if l < LEVELS else 16)
                if l >= 2:
                    pool.wait_ge(z_done if l - 2 < LEVELS else g_done, 4 * (l - 1))
                parts = [(2, w_stage[:, 2, :, :])]
                if l < LEVELS:
                    chain(pool.tensor_tensor(w_stage[:, 0, :, :], w_stage[:, 0, :, :], w_stage[:, 1, :, :], ALU.subtract))
                    parts = [(0, w_stage[:, 1, :, :]), (1, w_stage[:, 0, :, :]), (2, w_stage[:, 2, :, :])]
                for i, part in parts:
                    pool.tensor_copy(w_hi[:, r, :, i * D:(i + 1) * D], part).then_inc(pool_chain, 1)
                    n[0] += 1
                pool.wait_ge(pool_chain, n[0])
                for i, part in parts:
                    pool.tensor_tensor(w_lo[:, r, :, i * D:(i + 1) * D], part,
                                       w_hi[:, r, :, i * D:(i + 1) * D].bitcast(f32), ALU.subtract)\
                        .then_inc(pool_chain, 1)
                    n[0] += 1
                pool.wait_ge(pool_chain, n[0])
                pool.sem_inc(w_split, 1)

            for l in range(LEVELS + 1):
                split_weights(l)

            pool.wait_ge(x1_ready, NT)
            pool.iota(iota_e[:], pattern=[[0, NT], [1, EXPERTS]], base=0, channel_multiplier=0,
                      allow_small_or_imprecise_dtypes=True).then_inc(ffn_consts, 1)
            pool.iota(node_id[:], pattern=[[P, NT]], base=0, channel_multiplier=1,
                      allow_small_or_imprecise_dtypes=True).then_inc(ffn_consts, 1)
            pool.iota(iota_s[:], pattern=[[1, SLOT_TILES], [0, EXPERTS]], base=0, channel_multiplier=0,
                      allow_small_or_imprecise_dtypes=True).then_inc(ffn_consts, 1)
            pool.memset(zeros_e[:], 0.0).then_inc(ffn_consts, 1)
            pool.iota(iota_slot[:], pattern=[[P, SLOT_TILES], [1, P]], base=0, channel_multiplier=0,
                      allow_small_or_imprecise_dtypes=True).then_inc(ffn_consts, 1)
            pool.wait_ge(route_ready, 1)
            tiles = pool.value_load(owner_i[0:1, SLOT_TILES:SLOT_TILES + 1], min_val=MIN_TILES, max_val=MAX_TILES)
            pool.wait_ge(y_stored, tiles * 16)
            pool.sem_inc(rows_stored, 1)
            pool.wait_ge(rows_stored, 1)
            for t in range(NT):
                rows = P if t < NT - 1 else LAST
                for k in range(2):
                    pool.indirect_dma_start(
                        out=y_back[0:rows, t, k, :], out_offset=None, in_=ys_dram,
                        in_offset=bass.IndirectOffsetOnAxis(ap=slot_idx[0:rows, k, t:t + 1], axis=0))\
                        .then_inc(y_in[t], 16)

        @block.scalar
        def _(act):
            act.wait_ge(var_ready, 1)
            act.activation(std[:], var_eps[:], ACT.Sqrt).then_inc(std_ready, 1)
            for i, (h, c) in enumerate(Z_OUT):
                act.wait_ge(ht_f_done, i + 1)
                a, b = HALVES[h]
                act.copy(ht_hi[:, c, a:b], ht_f[:, c, a:b]).then_inc(ht_hi_done, 1)

            def ys_upper(l, t):
                n = l * NT + t
                act.wait_ge(ys_done, n + 1)
                act.copy(ys_hi[:, t, :], bank[ys_bank(l, t)][:, :]).then_inc(ys_hi_done, 1)

            def write_turn(turn, g):
                for c in range(UNROLL):
                    pane = bank[c % 2][:, 0:NT * WD].rearrange("p (n w) -> p n w", n=NT)
                    start = window_start(act, g * UNROLL + c)
                    act.wait_ge(chunk_done, turn * UNROLL + (c + 1))
                    act.copy(a_f[:, :, ds(start, WD)], pane).then_inc(a_written, 1)
                    act.wait_ge(pane_free, turn * UNROLL + (c + 2))
                    act.copy(a_hi[:, :, ds(start, WD)], pane).then_inc(pane_free, 1)

            act.wait_ge(a_zeroed, 2)
            act.wait_ge(base_ready, 1)
            act.sem_inc(a_written, 1)
            act.sem_inc(pane_free, 2)
            for i in range(SEGMENTS):
                with act.Fori(i * TURNS // SEGMENTS, (i + 1) * TURNS // SEGMENTS) as g:
                    write_turn(g, g)
                if i:
                    for t in SEG_TILES[i - 1]:
                        ys_upper(0, t)
            n_passes = passes(act)
            with act.If(n_passes > 1):
                with act.Fori(1, n_passes) as v:
                    act.wait_ge(base_ready, v + 1)
                    act.sem_inc(pass_begun, 1)
                    with act.Fori(0, TURNS) as g:
                        write_turn(v * TURNS + g, g)
            act.drain().then_inc(a_complete, 1)

            for l in range(LEVELS):
                if l:
                    for t in range(NT):
                        ys_upper(l, t)
                for i, (h, c) in enumerate(Z_OUT):
                    act.wait_ge(ht_f_done, 4 * (l + 1) + i + 1)
                    a, b = HALVES[h]
                    act.copy(ht_hi[:, c, a:b], ht_f[:, c, a:b]).then_inc(ht_hi_done, 1)

            act.wait_ge(var_ready, 2)
            act.activation(std[:], var_eps[:], ACT.Sqrt).then_inc(std_ready, 1)
            for s in range(2):
                act.wait_ge(gathered, s + 1)
                if s:
                    act.wait_ge(up_done, s)
                act.copy(xt[:], gather_ps()).then_inc(xt_ready, 1)
                if s == 0:
                    act.wait_ge(pre_ready, 1)
                    act.activation(h_act[:], h_pre[:], ACT.Gelu).then_inc(act_ready, 1)
            act.wait_ge(route_ready, 1)
            tiles = act.value_load(owner_i[0:1, SLOT_TILES:SLOT_TILES + 1], min_val=MIN_TILES, max_val=MAX_TILES)
            with act.Fori(0, tiles) as s:
                act.wait_ge(pre_ready, s + 2)
                act.wait_ge(t_done, s + 1)
                act.activation(h_act[:], h_pre[:], ACT.Gelu).then_inc(act_ready, 1)
                act.wait_ge(gathered, s + 3)
                act.copy(xt[:], gather_ps()).then_inc(xt_ready, 1)

        @block.vector
        def _(dve):
            n = [0]

            def chain(ins):
                n[0] += 1
                ins.then_inc(vec, 1)
                dve.wait_ge(vec, n[0])

            def layer_norm_stats(tile_of, round_):
                for t in range(NT):
                    last = dve.bn_stats(stats[:, t, :], tile_of(t))
                chain(last)
                for t in range(NT):
                    last = dve.bn_aggr(mv[:, t, :], stats[:, t, :])
                chain(last)
                dve.tensor_scalar(var_eps[:], mv[:, :, 1], EPS, None, ALU.add).then_inc(var_ready, 1)
                dve.wait_ge(std_ready, round_)
                chain(dve.reciprocal(rstd[:], std[:]))
                chain(dve.tensor_tensor(newton[:], rstd[:], rstd[:], ALU.mult))
                chain(dve.tensor_tensor(newton[:], newton[:], var_eps[:], ALU.mult))
                chain(dve.tensor_scalar(newton[:], newton[:], -0.5, 1.5, ALU.mult, ALU.add))
                chain(dve.tensor_tensor(rstd[:], rstd[:], newton[:], ALU.mult))

            dve.wait_ge(edges_in, 32)
            dve.tensor_single_scalar(hi_nat[:], src_nat[:], 7, ALU.arith_shift_right).then_inc(vec, 1)
            chain_after = dve.tensor_single_scalar(lo_nat[:], src_nat[:], P - 1, ALU.bitwise_and)
            n[0] += 1
            chain(chain_after)
            dve.tensor_copy(edge_nat[:, 0, :, :], lo_nat[:]).then_inc(edge_nat_done, 1)
            dve.scalar_tensor_tensor(edge_nat[:, 1, :, :], hi_nat[:], float(KEY), dst_nat[:], ALU.mult, ALU.add)\
                .then_inc(edge_nat_done, 1)
            dve.wait_ge(chunks_in, 16)
            chain(dve.tensor_reduce(span[:, 0:1], dst_chunk[:], AX.X, ALU.min))
            chain(dve.tensor_reduce(span[:, 1:2], dst_chunk[:], AX.X, ALU.max))
            dve.wait_ge(consts, 1)
            for i in range(2):
                dve.tensor_scalar(span_diag[:, i, :], ident[0:CHUNKS, 0:CHUNKS], span[:, i:i + 1], None, ALU.mult)\
                    .then_inc(span_ready, 1)
            dve.wait_ge(edge_t_done, 1)
            cols = bank[0][0:EP, 0:2 * ET].rearrange("p (a t) -> p a t", a=2)
            dve.tensor_copy(edge_rel[:, 0, :], cols[:, 0, :]).then_inc(edge_col_done, 1)
            dve.tensor_copy(edge_key[:], cols[:, 1, :]).then_inc(edge_col_done, 1)
            dve.wait_ge(span_ps, 1)
            chain(dve.tensor_copy(span_bc[:], bank[1][:, 0:2 * CHUNKS].rearrange("p (a c) -> p a c", a=2)))

            def set_windows():
                dve.tensor_tensor(edge_rel[:, 1, :].rearrange("p (c i) -> p c i", i=CT),
                                  edge_key[:].rearrange("p (c i) -> p c i", i=CT),
                                  span_bc[0:EP, 0, :].unsqueeze(2).broadcast_to((EP, CHUNKS, CT)), ALU.subtract)
                dve.tensor_copy(base_i[:], span_bc[0:1, 0, :]).then_inc(base_ready, 1)

            chain(dve.tensor_tensor(width[:], span_bc[0:1, 1, :], span_bc[0:1, 0, :], ALU.subtract))
            chain(dve.tensor_reduce(widest[:], width[:], AX.X, ALU.max))
            dve.wait_ge(consts, 4)
            chain(dve.tensor_scalar(needed[:], steps[:], widest[:], None, ALU.is_le))
            chain(dve.tensor_reduce(meta[:, 0:1], needed[:], AX.X, ALU.add))
            chain(dve.tensor_scalar(covers[:], span_bc[0:CHUNKS, 0, :], span[:, 1:2], None, ALU.is_le))
            dve.scalar_tensor_tensor(covers[:], span_bc[0:CHUNKS, 0, :], span[:, 0:1], covers[:],
                                     ALU.is_ge, ALU.mult).then_inc(covers_ready, 1)
            dve.wait_ge(covers_ps, 1)
            chain(dve.tensor_reduce(cover_row[:, 0:1], bank[1][0:1, 128:128 + CHUNKS], AX.X, ALU.max))
            chain(dve.tensor_scalar(meta[:, 1:2], cover_row[:, 0:1], float(COVER), None, ALU.is_gt))
            chain(dve.tensor_copy(meta_i[:], meta[:]))
            set_windows()

            dve.wait_ge(x_in, 32)
            layer_norm_stats(lambda t: x_sb[:, t, :], 1)
            for t in range(NT):
                dve.tensor_scalar(xn[:, t, :], x_sb[:, t, :], mv[:, t, 0:1], rstd[:, t:t + 1],
                                  ALU.subtract, ALU.mult).then_inc(xn_ready, 1)

            def ht_lower(i):
                h, c = Z_OUT[i % 4]
                a, b = HALVES[h]
                dve.wait_ge(ht_hi_done, i + 1)
                dve.tensor_tensor(ht_lo[:, c, a:b], ht_f[:, c, a:b], ht_hi[:, c, a:b].bitcast(f32),
                                  ALU.subtract).then_inc(ht_ready, 1)

            def ys_lower(l, t):
                k = l * NT + t
                dve.wait_ge(ys_hi_done, k + 1)
                dve.tensor_tensor(ys_lo[:, t, :], bank[ys_bank(l, t)][:, :], ys_hi[:, t, :].bitcast(f32),
                                  ALU.subtract).then_inc(ys_ready, 1)

            for i, (h, c) in enumerate(Z_OUT):
                dve.wait_ge(xn_t_done, i + 1)
                a, b = HALVES[h]
                dve.tensor_copy(ht_f[:, c, a:b], bank[i][:, 0:b - a]).then_inc(ht_f_done, 1)
            for i in range(4):
                ht_lower(i)

            def hot_turn(turn, g):
                dve.tensor_copy(edge_turn[:], edge_rel[:, :, ds(g * (UNROLL * CT), UNROLL * CT)])\
                    .then_inc(turn_ready, 1)
                dve.wait_ge(turn_ready, turn + 1)
                for c in range(UNROLL):
                    dve.wait_ge(chunk_free, turn * UNROLL + (c + 1))
                    for i in range(c * CT, (c + 1) * CT):
                        dve.tensor_scalar(hot_lo[:, i, :], iota_lo[0:EP, :], edge_turn[:, 0, i:i + 1], None,
                                          ALU.is_equal)
                        last = dve.tensor_scalar(hot_key[:, i, :, :], iota_key[0:EP], edge_turn[:, 1, i:i + 1],
                                                 None, ALU.is_equal)
                    last.then_inc(hot_chunk, 1)
                dve.wait_ge(hot_chunk, turn * UNROLL + UNROLL)

            dve.wait_ge(base_ready, 1)
            dve.wait_ge(edge_col_done, 2)
            for i in range(SEGMENTS):
                with dve.Fori(i * TURNS // SEGMENTS, (i + 1) * TURNS // SEGMENTS) as g:
                    hot_turn(g, g)
                if i:
                    for t in SEG_TILES[i - 1]:
                        ys_lower(0, t)
            n_passes = passes(dve)
            with dve.If(n_passes > 1):
                with dve.Fori(1, n_passes) as v:
                    dve.wait_ge(a_written, v * CHUNKS + 1)
                    dve.tensor_scalar(span_bc[:, 0, :], span_bc[:, 0, :], float(WD), float(NPAD),
                                      ALU.add, ALU.min).then_inc(window_moved, 1)
                    dve.wait_ge(window_moved, v)
                    set_windows()
                    dve.wait_ge(base_ready, v + 1)
                    dve.sem_inc(pass_begun, 1)
                    with dve.Fori(0, TURNS) as g:
                        hot_turn(v * TURNS + g, g)

            dve.wait_ge(cnt_done, 1)
            cnt = cnt_ps[:, 0:NPAD]
            dve.tensor_tensor(dg_f[:], cnt.rearrange("p (t m) -> p t m", t=NT),
                              ident[:].unsqueeze(1).broadcast_to((P, NT, P)), ALU.mult).then_inc(dg_done, 1)
            dve.tensor_scalar(rdeg[:], cnt, 1.0, None, ALU.max).then_inc(dg_done, 1)
            dve.wait_ge(dg_done, 2)
            dve.tensor_copy(dg_hi[:], dg_f[:]).then_inc(dg_done, 1)
            chain(dve.reciprocal(rdeg[:], rdeg[:]))

            for l in range(LEVELS):
                if l:
                    for t in range(NT):
                        ys_lower(l, t)
                for i, (h, c) in enumerate(Z_OUT):
                    a, b = HALVES[h]
                    dve.wait_ge(z_done, 4 * l + i + 1)
                    dve.scalar_tensor_tensor(ht_f[:, c, a:b], bank[i][:, 0:b - a], 0.0, rdeg[:, a:b],
                                             ALU.max, ALU.mult).then_inc(ht_f_done, 1)
                    ht_lower(4 * (l + 1) + i)

            dve.wait_ge(g_done, 1)
            for t in range(NT):
                dve.tensor_tensor(x1_sb[:, t, :], g_tile(t), x_sb[:, t, :], ALU.add).then_inc(x1_ready, 1)
            dve.wait_ge(x1_ready, NT)
            layer_norm_stats(lambda t: x1_sb[:, t, :], 2)
            for t in range(NT):
                dve.tensor_scalar(x2[:, t, :], x1_sb[:, t, :], mv[:, t, 0:1], rstd[:, t:t + 1],
                                  ALU.subtract, ALU.mult).then_inc(x2_ready, 1)
            dve.wait_ge(x2_ready, NT)
            chain(dve.tensor_copy(x2_hi[:], x2[:]))
            chain(dve.tensor_tensor(x2_lo[:], x2[:], x2_hi[:].bitcast(f32), ALU.subtract))
            for i in range(NT):
                dve.wait_ge(x2_t_ps, i + 1)
                dve.tensor_copy(x2_t[:, :, i * P:(i + 1) * P],
                                bank[i % 2][:, 0:D].rearrange("p (k s) -> p k s", k=KC)).then_inc(x2_t_ready, 1)
            dve.wait_ge(score_ps, 1)
            chain(dve.tensor_copy(score[:], bank[4][:, 0:NT * EXPERTS].rearrange("p (t e) -> p t e", t=NT)))
            for t in range(NT):
                last = dve.max(best[:, t, :], score[:, t, :])
            chain(last)
            for t in range(NT):
                last = dve.max_index(best_id[:, t, :], best[:, t, :], score[:, t, :])
            chain(last)
            chain(dve.tensor_copy(best_f[:], best_id[:, :, 0:2]))
            dve.wait_ge(ffn_consts, 5)
            chain(dve.tensor_scalar(valid[:], node_id[:], float(NODES), None, ALU.is_lt))
            for k in range(2):
                last = dve.tensor_tensor(pick[:, k, :, :], iota_e[:], best_f[:, :, k:k + 1].broadcast_to((P, NT, EXPERTS)),
                                         ALU.is_equal)
            chain(last)
            chain(dve.tensor_tensor(both[:], pick[:, 0, :, :], pick[:, 1, :, :], ALU.add))
            chain(dve.tensor_tensor(both[:], both[:], valid[:].unsqueeze(2).broadcast_to((P, NT, EXPERTS)), ALU.mult))
            dve.tensor_copy(both_bf[:], both[:]).then_inc(both_ready, 1)
            dve.wait_ge(prefix_ps, 1)
            sums = bank[4][:, 128:128 + NT * EXPERTS].rearrange("p (t e) -> p t e", t=NT)
            before = bank[4][:, 256:256 + NT * EXPERTS].rearrange("p (t e) -> p t e", t=NT)
            chain(dve.tensor_copy(tile_sum[:, 0, :], zeros_e[:]))
            for t in range(NT):
                chain(dve.tensor_tensor(tile_sum[:, t + 1, :], tile_sum[:, t, :], sums[:, t, :], ALU.add))
            chain(dve.tensor_scalar(tiles_i[:, 0, :], tile_sum[:, NT, :], float(P - 1), None, ALU.add))
            chain(dve.tensor_single_scalar(tiles_i[:, 1, :], tiles_i[:, 0, :], 7, ALU.arith_shift_right))
            chain(dve.tensor_copy(tiles_f[:], tiles_i[:, 1, :]))
            chain(dve.tensor_tensor_scan(tiles_end[:], tiles_f[:], zeros_e[:], 0.0, ALU.add, ALU.add))
            chain(dve.tensor_tensor(slot0[:], tiles_end[:], tiles_f[:], ALU.subtract))
            chain(dve.tensor_scalar(slot0[:], slot0[:], float(P), None, ALU.mult))
            chain(dve.tensor_tensor(slot[:], before, tile_sum[:, 0:NT, :], ALU.add))
            chain(dve.tensor_tensor(slot[:], slot[:], slot0[:].unsqueeze(1).broadcast_to((P, NT, EXPERTS)), ALU.add))
            chain(dve.scalar_tensor_tensor(slot_hot[:], slot[:].rearrange("p t e -> p e t"), 1.0,
                                           both[:].rearrange("p t e -> p e t"), ALU.add, ALU.mult))
            chain(dve.tensor_scalar(slot_hot[:], slot_hot[:], 1.0, None, ALU.subtract))
            chain(dve.tensor_tensor(past[:], iota_s[:], tiles_end[0:1, :].unsqueeze(1)
                                    .broadcast_to((1, SLOT_TILES, EXPERTS)), ALU.is_ge))
            chain(dve.tensor_reduce(owner[:, 0:SLOT_TILES], past[:], AX.X, ALU.add))
            chain(dve.tensor_scalar(owner[:, 0:SLOT_TILES], owner[:, 0:SLOT_TILES], float(EXPERTS - 1), None, ALU.min))
            chain(dve.tensor_copy(owner[:, SLOT_TILES:], tiles_end[0:1, EXPERTS - 1:EXPERTS]))
            dve.tensor_copy(owner_i[:], owner[:]).then_inc(route_ready, 1)

            def expert_of(s):
                return dve.value_load(owner_i[0:1, ds(s, 1)], min_val=0, max_val=EXPERTS - 1)

            def one_hot(s):
                e = expert_of(s)
                for t in range(NT):
                    last = dve.tensor_scalar(hot_slot[:, t, :], iota_slot[:, ds(s, 1), :], slot_hot[:, ds(e, 1), t],
                                             None, ALU.is_equal)
                last.then_inc(hot_ready, 1)

            def add_b1(s):
                e = expert_of(s)
                dve.tensor_tensor(h_pre[:], bank[1][:, :], b1_bc[:, ds(e, 1), :], ALU.add).then_inc(pre_ready, 1)

            dve.wait_ge(route_ready, 1)
            one_hot(0)
            dve.wait_ge(gathered, 1)
            one_hot(1)
            for k in range(2):
                last = dve.tensor_tensor(slot_pick[:, k, :, :], pick[:, k, :, :], slot[:], ALU.mult)
            chain(last)
            chain(dve.tensor_reduce(slot_of[:], slot_pick[:], AX.X, ALU.add))
            chain(dve.tensor_copy(slot_idx[:], slot_of[:]))
            dve.sem_inc(route_ready, 1)
            dve.wait_ge(ffn_b_in, 16 * (EXPERTS + 1))
            dve.wait_ge(up_done, 1)
            add_b1(0)
            dve.wait_ge(gathered, 2)
            one_hot(2)
            tiles = dve.value_load(owner_i[0:1, SLOT_TILES:SLOT_TILES + 1], min_val=MIN_TILES, max_val=MAX_TILES)
            with dve.Fori(0, tiles) as s:
                dve.wait_ge(t_done, s + 1)
                dve.tensor_copy(h_t[:], bank[2].rearrange("p (k s) -> p k s", k=HC)).then_inc(h_t_ready, 1)
                dve.wait_ge(up_done, s + 2)
                dve.wait_ge(act_ready, s + 1)
                add_b1(s + 1)
                dve.wait_ge(gathered, s + 3)
                one_hot(s + 3)
                e = expert_of(s)
                dve.wait_ge(down_done, s + 1)
                dve.tensor_tensor(y_sb[:, ds(s, 1), :], bank[3][:, 0:D], b2_bc[:, ds(e, 1), :], ALU.add)\
                    .then_inc(y_ready, 1)
            for t in range(NT):
                dve.wait_ge(y_in[t], 32)
                rows = P if t < NT - 1 else LAST
                chain(dve.tensor_tensor(x1_sb[0:rows, t, :], x1_sb[0:rows, t, :], y_back[0:rows, t, 0, :], ALU.add))
                dve.tensor_tensor(x1_sb[0:rows, t, :], x1_sb[0:rows, t, :], y_back[0:rows, t, 1, :], ALU.add)\
                    .then_inc(out_ready, 1)

        @block.tensor
        def _(pe):
            def exact3(out_, lhs, rhs, first, last):
                (lh, ll), (rh, rl) = lhs, rhs
                pe.matmul(out_, lh, rh, start=first, stop=False, skip_group_check=True)
                pe.matmul(out_, lh, rl, start=False, stop=False, skip_group_check=True)
                return pe.matmul(out_, ll, rh, start=False, stop=last, skip_group_check=True)

            pe.wait_ge(consts, 1)
            pe.wait_ge(edge_nat_done, 2)
            for a in range(2):
                for j in range(EH):
                    o = a * ET + j * EQ
                    last = pe.transpose(bank[0][0:EP, o:o + EQ], edge_nat[:, a, j, :], ident[0:EQ, 0:EQ])
            last.then_inc(edge_t_done, 1)
            pe.wait_ge(consts, 6)
            pe.wait_ge(span_ready, 2)
            pe.matmul(bank[1][:, 0:2 * CHUNKS], ones_sq[0:CHUNKS, :].bitcast(f32),
                      span_diag[:].rearrange("q a c -> q (a c)"), start=True, stop=True).then_inc(span_ps, 1)
            pe.wait_ge(covers_ready, 1)
            pe.matmul(bank[1][:, 128:128 + CHUNKS], ones_sq[0:CHUNKS, :].bitcast(f32), covers[:],
                      start=True, stop=True).then_inc(covers_ps, 1)
            pe.wait_ge(edge_t_done, 1)
            for i, (h, c) in enumerate(Z_OUT):
                a, b = HALVES[h]
                if i == 0:
                    pe.wait_ge(edge_col_done, 2)
                if i == 1:
                    pe.wait_ge(base_ready, 1)
                for t in range(a // P, b // P):
                    pe.wait_ge(xn_ready, t + 1)
                    last = pe.transpose(bank[i][:, t * P - a:(t + 1) * P - a], xn[:, t, c * P:(c + 1) * P], ident[:])
                last.then_inc(xn_t_done, 1)

            def ys_product(l, t):
                r, cols, o = l % 2, slice(t * P, (t + 1) * P), bank[ys_bank(l, t)]
                for k in range(KC):
                    exact3(o[:, :], (ht_hi[:, k, cols], ht_lo[:, k, cols]),
                           (w_hi[:, r, k, 0:2 * D], w_lo[:, r, k, 0:2 * D]), k == 0, False)
                pe.matmul(o[:, D:2 * D], row_pick[:, l, :], b_hi[:], start=False, stop=False,
                          skip_group_check=True)
                pe.matmul(o[:, D:2 * D], row_pick[:, l, :], b_lo[:], start=False, stop=True,
                          skip_group_check=True).then_inc(ys_done, 1)

            def g_product(l, t):
                r, cols = l % 2, slice(t * P, (t + 1) * P)
                for k in range(KC):
                    last = exact3(g_tile(t), (ht_hi[:, k, cols], ht_lo[:, k, cols]),
                                  (w_hi[:, r, k, 2 * D:], w_lo[:, r, k, 2 * D:]), False,
                                  l == LEVELS and k == KC - 1)
                return last

            pe.wait_ge(b_split, 2)
            for t in range(NT):
                pe.matmul(g_tile(t), row_pick[:, LEVELS, :], b_hi[:], start=t % 2 == 0, stop=False,
                          skip_group_check=True)
                pe.matmul(g_tile(t), row_pick[:, LEVELS, :], b_lo[:], start=False, stop=False,
                          skip_group_check=True)

            def sum_turn(turn, g):
                for c in range(UNROLL):
                    pane = bank[c % 2][:, 0:NT * WD]
                    start = window_start(pe, g * UNROLL + c)
                    pe.wait_ge(pane_free, turn * UNROLL + (c + 1))
                    pe.wait_ge(hot_chunk, turn * UNROLL + (c + 1))
                    for i in range(c * CT, (c + 1) * CT):
                        last = pe.matmul(pane, hot_lo[:, i, :], hot_key[:, i, :, :].rearrange("p n w -> p (n w)"),
                                         start=i == c * CT, stop=False, skip_group_check=True)
                    last.then_inc(chunk_free, 1)
                    pe.wait_ge(a_written, turn * UNROLL + (c + 1))
                    pe.matmul(pane, ident[:], a_f[:, :, ds(start, WD)], start=False, stop=True,
                              skip_group_check=True).then_inc(chunk_done, 1)

            pe.wait_ge(consts, 8)
            pe.wait_ge(base_ready, 1)
            pe.wait_ge(a_zeroed, 2)
            pe.wait_ge(ht_f_done, 4)
            pe.sem_inc(chunk_free, UNROLL)
            for i in range(SEGMENTS):
                with pe.Fori(i * TURNS // SEGMENTS, (i + 1) * TURNS // SEGMENTS) as g:
                    sum_turn(g, g)
                if i == 0:
                    pe.wait_ge(w_split, 1)
                    pe.wait_ge(ht_ready, 4)
                for t in SEG_TILES[i]:
                    if t >= 3:
                        pe.wait_ge(ys_ready, t - 2)
                    ys_product(0, t)
            n_passes = passes(pe)
            with pe.If(n_passes > 1):
                with pe.Fori(1, n_passes) as v:
                    pe.wait_ge(base_ready, v + 1)
                    pe.sem_inc(pass_begun, 1)
                    with pe.Fori(0, TURNS) as g:
                        sum_turn(v * TURNS + g, g)
            large = pe.value_load(meta_i[0:1, 1:2], min_val=0, max_val=1)
            pe.wait_ge(a_complete, 1)
            pe.wait_ge(ys_ready, NT)
            parts = [slice(0, 512), slice(512, NPAD)]

            def degrees(ones, a_t):
                for cols in parts:
                    for u in range(NT):
                        last = pe.matmul(cnt_ps[:, cols], ones, a_t[:, u, cols], start=u == 0, stop=u == NT - 1,
                                         skip_group_check=True)
                last.then_inc(cnt_done, 1)

            with pe.If(large > 0):
                degrees(ones_sq[:].bitcast(f32), a_f)
            with pe.Else():
                degrees(ones_sq[:], a_hi)

            for l in range(LEVELS):
                if l:
                    pe.wait_ge(w_split, l + 1)
                    for t in range(NT):
                        pe.wait_ge(ht_ready, 4 * l + (2 if t < 3 else 4))
                        if t >= 2:
                            pe.wait_ge(ys_ready, l * NT + t - 1)
                        ys_product(l, t)
                for t in range(NT):
                    g_product(l, t)

                def z_sums(y_parts, a_t, dg_t):
                    for i, (h, c) in enumerate(Z_OUT):
                        a, b = HALVES[h]
                        o = bank[i]
                        m = slice(c * P, (c + 1) * P)
                        ms = slice(D + c * P, D + (c + 1) * P)
                        for u in range(NT):
                            if i == 0:
                                pe.wait_ge(ys_ready, l * NT + (u + 1 if l == 0 else max(u + 1, NT - 1)))
                            for y in y_parts:
                                pe.matmul(o[:, 0:b - a], y[:, u, m], a_t[:, u, a:b], start=u == 0 and y is y_parts[0],
                                          stop=False, skip_group_check=True)
                        if l == 0 and i == 0:
                            pe.wait_ge(dg_done, 3)
                        for j in range(a // P, b // P):
                            for y in y_parts:
                                last = pe.matmul(o[:, j * P - a:(j + 1) * P - a], y[:, j, ms], dg_t[:, j, :],
                                                 start=False, stop=j == b // P - 1 and y is y_parts[-1],
                                                 skip_group_check=True)
                        last.then_inc(z_done, 1)

                with pe.If(large > 0):
                    z_sums([ys_hi[:].bitcast(f32), ys_lo[:].bitcast(f32)], a_f, dg_f)
                with pe.Else():
                    z_sums([ys_hi, ys_lo], a_hi, dg_hi)
            pe.wait_ge(w_split, LEVELS + 1)
            for t in range(NT):
                pe.wait_ge(ht_ready, 4 * LEVELS + (2 if t < 3 else 4))
                last = g_product(LEVELS, t)
            last.then_inc(g_done, 1)

            for t in range(NT):
                pe.wait_ge(x2_ready, t + 1)
                if t >= 2:
                    pe.wait_ge(x2_t_ready, t - 1)
                for k in range(KC):
                    last = pe.transpose(bank[t % 2][:, k * P:(k + 1) * P], x2[:, t, k * P:(k + 1) * P], ident[:])
                last.then_inc(x2_t_ps, 1)
            pe.wait_ge(ffn_w_in, 16 * (2 + 2 * EXPERTS))
            for t in range(NT):
                pe.wait_ge(x2_t_ready, t + 1)
                o = bank[4][:, t * EXPERTS:(t + 1) * EXPERTS]
                for k in range(KC):
                    pe.matmul(o, x2_t[:, k, t * P:(t + 1) * P], wg_sb[:, k, :], start=k == 0, stop=False,
                              skip_group_check=True)
                last = pe.matmul(o, ones_rowf[:], bg_row[:], start=False, stop=True, skip_group_check=True)
            last.then_inc(score_ps, 1)
            pe.wait_ge(both_ready, 1)
            picked = both_bf[:].rearrange("p t e -> p (t e)")
            pe.matmul(bank[4][:, 128:128 + NT * EXPERTS], ones_bf[:], picked, start=True, stop=True)
            pe.matmul(bank[4][:, 256:256 + NT * EXPERTS], tri_bf[:], picked, start=True, stop=True)\
                .then_inc(prefix_ps, 1)

            def gather(s):
                pe.wait_ge(hot_ready, s + 1)
                for k in range(KC):
                    o = bank[0][:, k * P:(k + 1) * P]
                    for t in range(NT):
                        pe.matmul(o, x2_hi[:, t, k * P:(k + 1) * P], hot_slot[:, t, :], start=t == 0, stop=False,
                                  skip_group_check=True)
                        last = pe.matmul(o, x2_lo[:, t, k * P:(k + 1) * P], hot_slot[:, t, :], start=False,
                                         stop=t == NT - 1, skip_group_check=True)
                last.then_inc(gathered, 1)

            def up(s):
                e = pe.value_load(owner_i[0:1, ds(s, 1)], min_val=0, max_val=EXPERTS - 1)
                pe.wait_ge(xt_ready, s + 1)
                for k in range(KC):
                    last = pe.matmul(bank[1][:, :], xt[:, k, :], w1_sb[:, ds(e, 1), k, :], start=k == 0,
                                     stop=k == KC - 1)
                last.then_inc(up_done, 1)

            pe.wait_ge(route_ready, 1)
            gather(0)
            pe.wait_ge(xt_ready, 1)
            gather(1)
            up(0)
            tiles = pe.value_load(owner_i[0:1, SLOT_TILES:SLOT_TILES + 1], min_val=MIN_TILES, max_val=MAX_TILES)
            with pe.Fori(0, tiles) as s:
                pe.wait_ge(act_ready, s + 1)
                for k in range(HC):
                    last = pe.transpose(bank[2][:, k * P:(k + 1) * P], h_act[:, k * P:(k + 1) * P], ident[:])
                last.then_inc(t_done, 1)
                up(s + 1)
                e = pe.value_load(owner_i[0:1, ds(s, 1)], min_val=0, max_val=EXPERTS - 1)
                pe.wait_ge(h_t_ready, s + 1)
                for k in range(HC):
                    last = pe.matmul(bank[3][:, 0:D], h_t[:, k, :], w2_sb[:, ds(e, 1), k, :], start=k == 0,
                                     stop=k == HC - 1)
                last.then_inc(down_done, 1)
                gather(s + 2)


_INS = ["x", "src", "dst"] + [f"L0_gnn_{n}" for n in ("W0", "b0", "W1", "b1", "W2", "b2", "Wf", "bf")] \
    + [f"L0_ffn_{n}" for n in ("Wg", "bg", "W1", "b1", "W2", "b2")]


def kernel(**inputs):
    import concourse.bacc as bacc
    from concourse.bass_utils import run_bass_kernel_spmd

    nc = bacc.Bacc("TRN2", target_bir_lowering=False, num_devices=1)
    arrays, ap = {}, {}
    for name in _INS:
        a = np.ascontiguousarray(inputs[name])
        arrays[f"in_{name}"] = a
        ap[name] = nc.dram_tensor(f"in_{name}", a.shape, mybir.dt.from_np(a.dtype), kind="ExternalInput").ap()
    out = nc.dram_tensor("out_rows", (NODES, D), mybir.dt.float32, kind="ExternalOutput").ap()
    g = {n: ap[f"L0_gnn_{n}"] for n in ("W0", "b0", "W1", "b1", "W2", "b2", "Wf", "bf")}
    f = {n: ap[f"L0_ffn_{n}"] for n in ("Wg", "bg", "W1", "b1", "W2", "b2")}
    build(nc, ap["x"], ap["src"], ap["dst"], [g["W0"], g["W1"], g["W2"]], [g["b0"], g["b1"], g["b2"]],
          g["Wf"], g["bf"], f["Wg"], f["bg"], f["W1"], f["b1"], f["W2"], f["b2"], out)
    r = run_bass_kernel_spmd(nc, [arrays], core_ids=[0])
    return r.results[0]["out_rows"]
```

```python
import concourse.bass as bass
from concourse import mybir
from contextlib import ExitStack
import numpy as np

NODES = 625
EDGES = 20000
D = 256
LEVELS = 3
EXPERTS = 8
HID = 512
EPS = 1e-5

P = 128
NT = -(-NODES // P)
NPAD = NT * P
LAST = NODES - (NT - 1) * P
KC = D // P
HC = HID // P

EP = 125
ET = EDGES // EP
EH = 2
EQ = ET // EH
assert EP * ET == EDGES and EQ * EH == ET and EQ <= P

CT = 4
CHUNKS = ET // CT
UNROLL = 8
RING = 4
TURNS = CHUNKS // UNROLL
WD = 36
AW = NPAD + WD
MAX_PASSES = -(-NODES // WD)
LOW = 32
BR = LOW + LEVELS + 1
KEY = 1024
assert 2 * CT * EP < 4096
SEGMENTS = [0, 2, 4, TURNS]
SEG_TILES = [[0, 1], [2], [3, 4]]

WARM_DEGREE, WARM_NORM, WARM_GATE, WARM_ROUTE, WARM_GATHER = 10, 12, 4, 10, 24

MAX_TILES = (2 * NODES + EXPERTS * (P - 1)) // P
MIN_PAIRS = -(-2 * NODES // P) // 2
MAX_PAIRS = MAX_TILES // 2
SLOT_TILES = 2 * (MAX_PAIRS + 2)
SPARE = NODES


def build(nc, x, src, dst, W, B, Wf, bf, Wg, bg, W1, b1, W2, b2, out):
    f32, f32r = mybir.dt.float32, mybir.dt.float32r
    bf16, i32, i16, u32 = mybir.dt.bfloat16, mybir.dt.int32, mybir.dt.int16, mybir.dt.uint32
    ALU = mybir.AluOpType
    ACT = mybir.ActivationFunctionType
    AX = mybir.AxisListType
    ds = bass.ds

    ctx = ExitStack()
    with ctx:
        def sb(name, shape, dt, scope=ctx):
            return scope.enter_context(nc.sbuf_tensor(name, shape, dt))

        def sem(name):
            return ctx.enter_context(nc.semaphore(name))

        w1_sb = sb("w1_sb", [P, EXPERTS, KC, HID], f32)
        w2_sb = sb("w2_sb", [P, EXPERTS, HC, D], f32)
        wg_sb = sb("wg_sb", [P, KC, EXPERTS], f32)
        bg_bc = sb("bg_bc", [P, EXPERTS], f32)
        x_sb = sb("x_sb", [P, NT, D], f32)
        x1_sb = sb("x1_sb", [P, NT, D], f32)
        ident = sb("ident", [P, P], f32)
        ones_sq = sb("ones_sq", [P, P], f32r)
        ones_bf = sb("ones_bf", [P, P], bf16)
        tri_bf = sb("tri_bf", [P, P], bf16)
        stats = sb("stats", [P, NT, 6], f32)
        mv = sb("mv", [P, NT, 2], f32)
        std = sb("std", [P, NT], f32)
        rstd = sb("rstd", [P, NT], f32)
        var_eps = sb("var_eps", [P, NT], f32)
        newton = sb("newton", [P, NT], f32)
        iota_lo = sb("iota_lo", [P, P, CT], i16)

        gnn = ExitStack()
        w_stage = sb("w_stage", [P, 3, KC, D], f32, gnn)
        w_hi = sb("w_hi", [P, 2, KC, 3 * D], f32r, gnn)
        w_lo = sb("w_lo", [P, 2, KC, 3 * D], f32r, gnn)
        b_rows = sb("b_rows", [BR, D], f32, gnn)
        b_split = sb("b_split", [BR, D], f32r, gnn)
        row_pick = sb("row_pick", [BR, LEVELS + 1, P], f32r, gnn)
        a_f = sb("a_f", [P, NT, AW], f32, gnn)
        a_hi = sb("a_hi", [P, NT, AW], f32r, gnn)
        rdeg = sb("rdeg", [P, NPAD], f32, gnn)
        cnt_f = sb("cnt_f", [P, NPAD], f32, gnn)
        cnt_r = sb("cnt_r", [BR, NPAD], f32r, gnn)
        diag = sb("diag", [P, NT, P], f32, gnn)
        deg_col = sb("deg_col", [P, NT], f32, gnn)
        rdeg_col = sb("rdeg_col", [P, NT], f32, gnn)
        b_level = sb("b_level", [BR, LEVELS, D], f32r, gnn)
        ut_hi = sb("ut_hi", [P, KC, NPAD], f32r, gnn)
        ut_lo = sb("ut_lo", [P, KC, NPAD], f32r, gnn)
        ht_f = sb("ht_f", [P, KC, NPAD], f32, gnn)
        ht_hi = sb("ht_hi", [P, KC, NPAD], f32r, gnn)
        ht_lo = sb("ht_lo", [P, KC, NPAD], f32r, gnn)
        ys_hi = sb("ys_hi", [P, NT, D], f32r, gnn)
        ys_lo = sb("ys_lo", [P, NT, D], f32r, gnn)
        xn = x1_sb
        src_nat = sb("src_nat", [EQ, EH, EP], i32, gnn)
        dst_nat = sb("dst_nat", [EQ, EH, EP], i32, gnn)
        dst_chunk = sb("dst_chunk", [CHUNKS, CT * EP], i32, gnn)
        hi_nat = sb("hi_nat", [EQ, EH, EP], i32, gnn)
        lo_nat = sb("lo_nat", [EQ, EH, EP], i32, gnn)
        edge_nat = sb("edge_nat", [EQ, 2, EH, EP], f32, gnn)
        edge_key = sb("edge_key", [EP, ET], f32, gnn)
        edge_rel = sb("edge_rel", [EP, 2, ET], i16, gnn)
        edge_turn = sb("edge_turn", [EP, 2, UNROLL * CT], i16, gnn)
        span = sb("span", [CHUNKS, 2], f32, gnn)
        span_diag = sb("span_diag", [CHUNKS, 2, CHUNKS], f32, gnn)
        span_bc = sb("span_bc", [P, 2, CHUNKS], f32, gnn)
        width = sb("width", [1, CHUNKS], f32, gnn)
        widest = sb("widest", [1, 1], f32, gnn)
        steps = sb("steps", [1, MAX_PASSES], f32, gnn)
        needed = sb("needed", [1, MAX_PASSES], f32, gnn)
        shared = sb("shared", [1, CHUNKS - 2], f32, gnn)
        any_shared = sb("any_shared", [1, 1], f32, gnn)
        meta = sb("meta", [1, 2], f32, gnn)
        meta_i = sb("meta_i", [1, 2], i32, gnn)
        base_i = sb("base_i", [1, CHUNKS], i32, gnn)
        iota_key = sb("iota_key", [P, NT * WD, CT], i16, gnn)
        hot_lo = sb("hot_lo", [EP, RING, P, CT], bf16, gnn)
        hot_key = sb("hot_key", [EP, RING, NT * WD, CT], bf16, gnn)
        gnn.close()

        ffn = ExitStack()
        b1_bc = sb("b1_bc", [P, EXPERTS, HID], f32, ffn)
        b2_bc = sb("b2_bc", [P, EXPERTS, D], f32, ffn)
        xc = sb("xc", [P, NT, D], f32, ffn)
        x2_hi = sb("x2_hi", [P, NT, D], f32r, ffn)
        x2_lo = sb("x2_lo", [P, NT, D], f32r, ffn)
        xc_t = sb("xc_t", [P, KC, NPAD], f32, ffn)
        score = sb("score", [P, NT, EXPERTS], f32, ffn)
        best = sb("best", [P, NT, 8], f32, ffn)
        best_id = sb("best_id", [P, NT, 8], u32, ffn)
        iota_e = sb("iota_e", [P, NT, EXPERTS], f32, ffn)
        node_id = sb("node_id", [P, NT], f32, ffn)
        valid = sb("valid", [P, NT], f32, ffn)
        pick = sb("pick", [P, 2, NT, EXPERTS], f32, ffn)
        both = sb("both", [P, NT, EXPERTS], f32, ffn)
        both_bf = sb("both_bf", [P, NT, EXPERTS], bf16, ffn)
        tiles_i = sb("tiles_i", [P, 2, EXPERTS], i32, ffn)
        tiles_f = sb("tiles_f", [P, EXPERTS], f32, ffn)
        tiles_end = sb("tiles_end", [P, EXPERTS], f32, ffn)
        zeros_e = sb("zeros_e", [P, EXPERTS], f32, ffn)
        slot0 = sb("slot0", [P, EXPERTS], f32, ffn)
        slot = sb("slot", [P, NT, EXPERTS], f32, ffn)
        slot_pick = sb("slot_pick", [P, 2, NT, EXPERTS], f32, ffn)
        slot_of = sb("slot_of", [P, 2, NT], f32, ffn)
        slot_i = sb("slot_i", [P, 2, NT], i32, ffn)
        pos_i = sb("pos_i", [P, 2, NT], i32, ffn)
        pos_f = sb("pos_f", [P, 2, NT], f32, ffn)
        slot_1 = sb("slot_1", [P, 2, NT], f32, ffn)
        from_tile = sb("from_tile", [P, 2, SLOT_TILES, NT], f32, ffn)
        in_tile = sb("in_tile", [P, 2, SLOT_TILES, NT], f32, ffn)
        hot_pos = sb("hot_pos", [P, SLOT_TILES, NT], f32, ffn)
        tile_start = sb("tile_start", [P, SLOT_TILES, NT], f32, ffn)
        pair_pos = sb("pair_pos", [P, 2, NT], f32, ffn)
        row_id = sb("row_id", [P, NT], f32, ffn)
        hot_place = sb("hot_place", [P, 2, NT, P], f32r, ffn)
        row_in_tile = sb("row_in_tile", [P, 2, SLOT_TILES, NT], f32r, ffn)
        spare_row = sb("spare_row", [P, 1], f32, ffn)
        unused = sb("unused", [P, SLOT_TILES], f32, ffn)
        row_of = sb("row_of", [P, SLOT_TILES], i32, ffn)
        row_now = sb("row_now", [P, 2], i32, ffn)
        iota_s = sb("iota_s", [P, SLOT_TILES], f32, ffn)
        past = sb("past", [1, SLOT_TILES, EXPERTS], f32, ffn)
        owner = sb("owner", [1, SLOT_TILES + 1], f32, ffn)
        owner_i = sb("owner_i", [1, SLOT_TILES + 1], i32, ffn)
        pairs_i = sb("pairs_i", [1, 2], i32, ffn)
        iota_p = sb("iota_p", [P, P], f32, ffn)
        hot_slot = sb("hot_slot", [P, NT, 2 * P], f32r, ffn)
        xt = sb("xt", [P, KC, 2 * P], f32, ffn)
        h_pre = sb("h_pre", [P, HID], f32, ffn)
        h_act = sb("h_act", [P, HID], f32, ffn)
        h_t = sb("h_t", [P, HC, P], f32, ffn)
        warm = sb("warm", [P, NT], f32, ffn)
        y_sb = sb("y_sb", [P, 2, D], f32, ffn)
        ffn.close()

        bank = [ctx.enter_context(nc.psum_tensor(f"bank{i}", [P, 512], f32)) for i in range(2)]
        cnt_ps = ctx.enter_context(nc.psum_tensor("cnt_ps", [P, 1024], f32))
        bank += [cnt_ps[:, 0:512], cnt_ps[:, 512:1024]]
        bank += [ctx.enter_context(nc.psum_tensor("bank4", [P, 512], f32))]
        g_ps = [ctx.enter_context(nc.psum_tensor(f"g_ps{i}", [P, 512], f32)) for i in range(3)]

        def g_tile(t):
            return g_ps[t // 2][:, (t % 2) * D:(t % 2) * D + D]

        edges_in = sem("edges_in")
        chunks_in = sem("chunks_in")
        x_in = sem("x_in")
        small_in = sem("small_in")
        w_in = [sem(f"w_in{l}") for l in range(LEVELS + 1)]
        ffn_w_in = sem("ffn_w_in")
        ffn_b_in = sem("ffn_b_in")
        consts = sem("consts")
        x_zeroed = sem("x_zeroed")
        pool_chain = sem("pool_chain")
        w_split = sem("w_split")
        b_zeroed = sem("b_zeroed")
        b_ready = sem("b_ready")
        ffn_consts = sem("ffn_consts")
        vec = sem("vec")
        edge_nat_done = sem("edge_nat_done")
        span_ready = sem("span_ready")
        span_ps = sem("span_ps")
        edge_t_done = sem("edge_t_done")
        edge_col_done = sem("edge_col_done")
        base_ready = sem("base_ready")
        a_zeroed = sem("a_zeroed")
        window_moved = sem("window_moved")
        pass_begun = sem("pass_begun")
        var_ready = sem("var_ready")
        std_ready = sem("std_ready")
        rstd_ready = sem("rstd_ready")
        xn_ready = sem("xn_ready")
        xn_t_done = sem("xn_t_done")
        ht_hi_done = sem("ht_hi_done")
        ht_f_done = sem("ht_f_done")
        h0_copied = sem("h0_copied")
        g_added = sem("g_added")
        ht_ready = sem("ht_ready")
        turn_ready = sem("turn_ready")
        hot_chunk = sem("hot_chunk")
        chunk_free = sem("chunk_free")
        chunk_done = sem("chunk_done")
        a_written = sem("a_written")
        meta_ready = sem("meta_ready")
        a_complete = sem("a_complete")
        a_added = sem("a_added")
        a_added_pool = sem("a_added_pool")
        cnt_done = sem("cnt_done")
        cnt_read = sem("cnt_read")
        rdeg_ready = sem("rdeg_ready")
        rdeg_ps = sem("rdeg_ps")
        u0_ready = sem("u0_ready")
        ut_hi_done = sem("ut_hi_done")
        ut_ready = sem("ut_ready")
        ys_done = sem("ys_done")
        ys_hi_done = sem("ys_hi_done")
        ys_ready = sem("ys_ready")
        z_done = sem("z_done")
        g_done = sem("g_done")
        x1_ready = sem("x1_ready")
        xc_ready = sem("xc_ready")
        x2_hi_done = sem("x2_hi_done")
        x2_lo_done = sem("x2_lo_done")
        xc_t_ps = sem("xc_t_ps")
        xc_t_ready = sem("xc_t_ready")
        score_ps = sem("score_ps")
        both_ready = sem("both_ready")
        prefix_ps = sem("prefix_ps")
        pair_taken = sem("pair_taken")
        hot_ready = sem("hot_ready")
        gathered = sem("gathered")
        xt_ready = sem("xt_ready")
        up_done = sem("up_done")
        pre_ready = sem("pre_ready")
        act_ready = sem("act_ready")
        t_done = sem("t_done")
        h_t_ready = sem("h_t_ready")
        down_done = sem("down_done")
        y_ready = sem("y_ready")
        experts_ready = sem("experts_ready")
        row_pairs_ready = sem("row_pairs_ready")
        row_ps = sem("row_ps")
        rows_ready = sem("rows_ready")
        row_taken = sem("row_taken")
        y_scattered = sem("y_scattered")
        y_landed = sem("y_landed")
        all_scattered = sem("all_scattered")
        pool_turn = sem("pool_turn")
        x1_stored = sem("x1_stored")

        block = ctx.enter_context(nc.Block())

        x_rows = x[0:(NT - 1) * P, :].rearrange("(t p) d -> p t d", p=P)
        HALVES = [(0, 3 * P), (3 * P, NPAD)]
        Z_OUT = [(h, c) for h in range(2) for c in range(KC)]
        Z_ORDER = (2, 3, 0, 1)

        def part(i):
            (h, c) = Z_OUT[i]
            return slice(*HALVES[h]), c

        def z_bank(i):
            return bank[i][:, 0:HALVES[Z_OUT[i][0]][1] - HALVES[Z_OUT[i][0]][0]]

        def rdeg_bank(h):
            return (bank[4][:, 0:HALVES[0][1]], g_ps[2][:, D:2 * D])[h]

        YS_ORDER = (3, 4, 0, 1, 2)

        def ys_bank(l, j):
            return bank[(4, 2, 3)[j % 3] if l == 0 else (4, 0, 1)[j % 3]][:, 0:D]

        DVE_ADDS = [(u, slice(0, NPAD)) for u in range(NT - 2)] + [(NT - 2, slice(0, NPAD // 2))]
        POOL_ADDS = [(NT - 1, slice(0, NPAD)), (NT - 2, slice(NPAD // 2, NPAD))]

        def gather_ps():
            return bank[0].rearrange("p (k s) -> p k s", k=KC)

        def pairs(eng):
            return eng.value_load(pairs_i[0:1, 0:1], min_val=MIN_PAIRS, max_val=MAX_PAIRS)

        def odd_tile(eng):
            return eng.value_load(pairs_i[0:1, 1:2], min_val=0, max_val=1)

        def expert_of(eng, s):
            return eng.value_load(owner_i[0:1, ds(s, 1)], min_val=0, max_val=EXPERTS - 1)

        def pane(c):
            return bank[c % 2][:, 0:NT * WD].rearrange("p (n w) -> p n w", n=NT)

        def pass_end(eng):
            return eng.value_load(meta_i[0:1, 0:1], min_val=2, max_val=MAX_PASSES + 1)

        def general(eng):
            return eng.value_load(meta_i[0:1, 1:2], min_val=0, max_val=1)

        def window_start(eng, c):
            return eng.value_load(base_i[0:1, ds(c, 1)], min_val=0, max_val=NPAD)

        @block.sync
        def _(sp):
            sp.dma_start(dst_nat[:], dst.rearrange("(j q e) -> q j e", j=EH, e=EP)).then_inc(edges_in, 16)
            sp.dma_start(src_nat[:], src.rearrange("(j q e) -> q j e", j=EH, e=EP)).then_inc(edges_in, 16)
            sp.dma_start(dst_chunk[:], dst.rearrange("(c e) -> c e", c=CHUNKS)).then_inc(chunks_in, 16)
            sp.wait_ge(x_zeroed, 1)
            sp.dma_start(x_sb[:, 0:NT - 1, :], x_rows).then_inc(x_in, 16)
            sp.dma_start(x_sb[0:LAST, NT - 1, :], x[(NT - 1) * P:NODES, :]).then_inc(x_in, 16)
            sp.wait_ge(b_zeroed, 1)
            for i, b in enumerate(B + [bf]):
                for row in (i, LOW + i):
                    sp.dma_start(b_rows[row:row + 1, :], b.unsqueeze(0)).then_inc(small_in, 16)
            for l in range(LEVELS + 1):
                if l:
                    sp.wait_ge(w_split, l)
                if l < LEVELS:
                    sp.dma_start(w_stage[:, 0:2, :, :],
                                 W[l].rearrange("(h k p) d -> p h k d", h=2, k=KC)).then_inc(w_in[l], 16)
                sp.dma_start(w_stage[:, 2, :, :],
                             Wf[l * D:(l + 1) * D, :].rearrange("(k p) d -> p k d", k=KC)).then_inc(w_in[l], 16)
            sp.dma_start(wg_sb[:], Wg.rearrange("(k p) e -> p k e", k=KC)).then_inc(ffn_w_in, 16)
            sp.dma_start(bg_bc[:], bg.partition_broadcast(P)).then_inc(ffn_w_in, 16)
            for e in range(EXPERTS):
                sp.dma_start(w1_sb[:, e, :, :], W1[e].rearrange("(k p) h -> p k h", k=KC)).then_inc(ffn_w_in, 16)
                sp.dma_start(w2_sb[:, e, :, :], W2[e].rearrange("(k p) d -> p k d", k=HC)).then_inc(ffn_w_in, 16)
            sp.wait_ge(x1_ready, NT)
            sp.dma_start(out[0:(NT - 1) * P, :].rearrange("(t p) d -> p t d", p=P), x1_sb[:, 0:NT - 1, :])\
                .then_inc(x1_stored, 16)
            sp.dma_start(out[(NT - 1) * P:NODES, :], x1_sb[0:LAST, NT - 1, :]).then_inc(x1_stored, 16)
            sp.dma_start(out[SPARE:, :], x1_sb[:, 0, :]).then_inc(x1_stored, 16)
            for e in range(EXPERTS):
                sp.dma_start(b1_bc[:, e, :], b1[e].partition_broadcast(P)).then_inc(ffn_b_in, 16)
            sp.dma_start(b2_bc[:], b2.rearrange("e d -> (e d)").partition_broadcast(P)
                         .rearrange("p (e d) -> p e d", e=EXPERTS)).then_inc(ffn_b_in, 16)
            sp.wait_ge(all_scattered, 1)

        @block.gpsimd
        def _(pool):
            n = [0]

            def chain(ins):
                n[0] += 1
                ins.then_inc(pool_chain, 1)
                pool.wait_ge(pool_chain, n[0])

            pool.memset(x_sb[:, NT - 1, :], 0.0).then_inc(x_zeroed, 1)
            pool.memset(b_rows[:], 0.0).then_inc(b_zeroed, 1)
            chain(pool.memset(ident[:], 0.0))
            pool.affine_select(out=ident[:], in_=ident[:], compare_op=ALU.not_equal, fill=1.0, base=0,
                               pattern=[[-1, P]], channel_multiplier=1).then_inc(consts, 1)
            pool.iota(iota_lo[:], pattern=[[1, P], [0, CT]], base=0, channel_multiplier=0,
                      allow_small_or_imprecise_dtypes=True).then_inc(consts, 1)
            pool.iota(iota_key[:].rearrange("p (n w) i -> p n w i", n=NT),
                      pattern=[[KEY, NT], [1, WD], [0, CT]], base=0, channel_multiplier=0,
                      allow_small_or_imprecise_dtypes=True).then_inc(consts, 1)
            pool.iota(steps[:], pattern=[[WD, MAX_PASSES]], base=0, channel_multiplier=0,
                      allow_small_or_imprecise_dtypes=True).then_inc(consts, 1)
            pool.memset(ones_sq[:].bitcast(f32), 1.0).then_inc(consts, 1)
            pool.memset(ones_bf[:], 1.0).then_inc(consts, 1)
            chain(pool.memset(tri_bf[:], 0.0))
            pool.affine_select(out=tri_bf[:], in_=tri_bf[:], compare_op=ALU.is_ge, fill=1.0, base=0,
                               pattern=[[-1, P]], channel_multiplier=1).then_inc(consts, 1)
            pool.memset(a_hi[:].bitcast(f32), 0.0).then_inc(a_zeroed, 1)
            pool.memset(a_f[:], 0.0).then_inc(a_zeroed, 1)
            pool.wait_ge(consts, 1)
            pool.tensor_tensor(row_pick[:], ident[0:BR, 0:LEVELS + 1].unsqueeze(2).broadcast_to((BR, LEVELS + 1, P)),
                               ident[0:BR, LOW:LOW + LEVELS + 1].unsqueeze(2).broadcast_to((BR, LEVELS + 1, P)),
                               ALU.add).then_inc(b_ready, 1)
            pool.wait_ge(small_in, 16 * 2 * (LEVELS + 1))
            chain(pool.tensor_copy(b_split[:], b_rows[:]))
            pool.tensor_tensor(b_split[LOW:, :], b_rows[LOW:, :], b_split[LOW:, :].bitcast(f32), ALU.subtract)\
                .then_inc(b_ready, 1)
            pool.wait_ge(b_ready, 2)
            for l in range(LEVELS):
                pool.tensor_tensor(b_level[:, l, :], b_split[:].bitcast(f32),
                                   row_pick[:, l, 0:1].bitcast(f32).broadcast_to((BR, D)), ALU.mult).then_inc(b_ready, 1)
                pool.wait_ge(b_ready, 3 + l)

            def split_weights(l):
                r = l % 2
                pool.wait_ge(w_in[l], 32 if l < LEVELS else 16)
                if l >= 2:
                    pool.wait_ge(z_done if l - 2 < LEVELS else g_done, 4 * (l - 1))
                parts = [(2, w_stage[:, 2, :, :])]
                if l < LEVELS:
                    chain(pool.tensor_tensor(w_stage[:, 0, :, :], w_stage[:, 0, :, :], w_stage[:, 1, :, :], ALU.subtract))
                    parts = [(0, w_stage[:, 1, :, :]), (1, w_stage[:, 0, :, :]), (2, w_stage[:, 2, :, :])]
                for i, part in parts:
                    pool.tensor_copy(w_hi[:, r, :, i * D:(i + 1) * D], part).then_inc(pool_chain, 1)
                    n[0] += 1
                pool.wait_ge(pool_chain, n[0])
                for i, part in parts:
                    pool.tensor_tensor(w_lo[:, r, :, i * D:(i + 1) * D], part,
                                       w_hi[:, r, :, i * D:(i + 1) * D].bitcast(f32), ALU.subtract)\
                        .then_inc(pool_chain, 1)
                    n[0] += 1
                pool.wait_ge(pool_chain, n[0])
                pool.sem_inc(w_split, 1)

            split_weights(0)
            split_weights(1)
            pool.wait_ge(a_complete, 1)
            for i, (u, cols) in enumerate(POOL_ADDS):
                pool.tensor_tensor(a_hi[:, u, cols], a_hi[:, u, cols].bitcast(f32), a_f[:, u, cols], ALU.add)\
                    .then_inc(a_added_pool, 1)
                pool.wait_ge(a_added_pool, i + 1)
            for l in range(2, LEVELS + 1):
                split_weights(l)

            pool.wait_ge(x1_ready, NT)
            pool.iota(iota_e[:], pattern=[[0, NT], [1, EXPERTS]], base=0, channel_multiplier=0,
                      allow_small_or_imprecise_dtypes=True).then_inc(ffn_consts, 1)
            pool.iota(node_id[:], pattern=[[P, NT]], base=0, channel_multiplier=1,
                      allow_small_or_imprecise_dtypes=True).then_inc(ffn_consts, 1)
            pool.memset(zeros_e[:], 0.0).then_inc(ffn_consts, 1)
            pool.iota(row_id[:], pattern=[[P, NT]], base=1, channel_multiplier=1,
                      allow_small_or_imprecise_dtypes=True).then_inc(ffn_consts, 1)
            pool.iota(iota_s[:], pattern=[[1, SLOT_TILES]], base=0, channel_multiplier=0,
                      allow_small_or_imprecise_dtypes=True).then_inc(ffn_consts, 1)
            pool.iota(iota_p[:], pattern=[[1, P]], base=1, channel_multiplier=0,
                      allow_small_or_imprecise_dtypes=True).then_inc(ffn_consts, 1)
            pool.iota(tile_start[:], pattern=[[P, SLOT_TILES], [0, NT]], base=0, channel_multiplier=0,
                      allow_small_or_imprecise_dtypes=True).then_inc(ffn_consts, 1)
            pool.iota(spare_row[:], pattern=[[0, 1]], base=SPARE + 1, channel_multiplier=1,
                      allow_small_or_imprecise_dtypes=True).then_inc(ffn_consts, 1)
            pool.sem_inc(y_landed, 2)
            pool.wait_ge(x1_stored, 48)
            pool.wait_ge(rows_ready, 1)
            n_pairs = pairs(pool)
            is_odd = odd_tile(pool)
            pool.tensor_copy(row_now[:], row_of[:, 0:2]).then_inc(row_taken, 1)
            pool.wait_ge(row_taken, 1)

            def scatter(s, h):
                pool.wait_ge(y_ready, s + 2)
                pool.sem_inc(pool_turn, 1)
                pool.indirect_dma_start(
                    out=out, out_offset=bass.IndirectOffsetOnAxis(ap=row_now[:, h:h + 1], axis=0),
                    in_=y_sb[:, h, :], in_offset=None, compute_op=ALU.add).then_inc(y_scattered, 16)
                pool.wait_ge(y_scattered, s * 16 + 16)
                pool.sem_inc(y_landed, 1)

            with pool.Fori(0, n_pairs) as p:
                for h in range(2):
                    scatter(p * 2 + h, h)
                pool.tensor_copy(row_now[:], row_of[:, ds(p * 2 + 2, 2)]).then_inc(row_taken, 1)
                pool.wait_ge(row_taken, p + 2)
            with pool.If(is_odd > 0):
                scatter(n_pairs * 2, 0)
            pool.sem_inc(all_scattered, 1)

        @block.scalar
        def _(act):
            act.wait_ge(var_ready, 1)
            act.activation(std[:], var_eps[:], ACT.Sqrt).then_inc(std_ready, 1)
            for i, (h, c) in enumerate(Z_OUT):
                act.wait_ge(xn_t_done, i + 1)
                a, b = HALVES[h]
                act.copy(ht_f[:, c, a:b], bank[i][:, 0:b - a]).then_inc(h0_copied, 1)
                act.copy(ht_hi[:, c, a:b], bank[i][:, 0:b - a]).then_inc(ht_hi_done, 1)

            def ys_upper(l, j):
                t = j if l == 0 else YS_ORDER[j]
                act.wait_ge(ys_done, l * NT + j + 1)
                if l == 0:
                    act.copy(ys_hi[:, t, :], ys_bank(l, j)).then_inc(ys_hi_done, 1)
                else:
                    act.activation(ys_hi[:, t, :], ys_bank(l, j), ACT.Copy, scale=rdeg_col[:, t:t + 1])\
                        .then_inc(ys_hi_done, 1)

            def write_turn(matrices, turn, g, summed, first):
                for c in range(UNROLL):
                    start = window_start(act, g * UNROLL + c)
                    act.wait_ge(a_written, turn * UNROLL + (c + 2))
                    act.wait_ge(summed, first + (c + 1))
                    act.copy(matrices[c % 2][:, :, ds(start, WD)], pane(c)).then_inc(a_written, 1)

            act.wait_ge(a_zeroed, 2)
            act.wait_ge(base_ready, 1)
            act.sem_inc(a_written, 2)
            for i in range(len(SEGMENTS) - 1):
                with act.Fori(SEGMENTS[i], SEGMENTS[i + 1]) as g:
                    write_turn((a_hi, a_f), g, g, chunk_free, g * UNROLL + RING)
                if i:
                    for t in SEG_TILES[i - 1]:
                        ys_upper(0, t)
            act.wait_ge(meta_ready, 1)
            with act.If(general(act) > 0):
                with act.Fori(1, pass_end(act)) as v:
                    act.wait_ge(base_ready, v + 1)
                    act.sem_inc(pass_begun, 1)
                    with act.Fori(0, TURNS) as g:
                        write_turn((a_f, a_f), v * TURNS + g, g, chunk_done, ((v - 1) * TURNS + g) * UNROLL)
            act.drain().then_inc(a_complete, 1)
            for t in SEG_TILES[-1]:
                ys_upper(0, t)

            act.wait_ge(cnt_read, 1)
            act.copy(cnt_r[:], cnt_f[0:BR, :]).then_inc(cnt_read, 1)
            for i in Z_ORDER:
                cols, c = part(i)
                act.wait_ge(u0_ready, c + 1)
                act.copy(ut_hi[:, c, cols], ht_f[:, c, cols]).then_inc(ut_hi_done, 1)

            for l in range(LEVELS):
                for j, i in enumerate(Z_ORDER):
                    cols, c = part(i)
                    if l == LEVELS - 1:
                        continue
                    act.wait_ge(z_done, 4 * l + j + 1)
                    act.activation(ut_hi[:, c, cols], z_bank(i), ACT.Relu).then_inc(ut_hi_done, 1)
                if l < LEVELS - 1:
                    for j in range(NT):
                        ys_upper(l + 1, j)
                to = ht_hi if l < LEVELS - 1 else ut_hi
                if l < LEVELS - 1:
                    act.wait_ge(g_added, l + 1)
                else:
                    act.wait_ge(z_done, 4 * l + 2)
                for j, i in enumerate(Z_ORDER):
                    cols, c = part(i)
                    act.wait_ge(ht_f_done, 4 * l + j + 1)
                    act.copy(to[:, c, cols], ht_f[:, c, cols]).then_inc(ht_hi_done, 1)

            act.wait_ge(var_ready, 2)
            act.activation(std[:], var_eps[:], ACT.Sqrt).then_inc(std_ready, 1)
            for i in range(NT):
                act.wait_ge(xc_t_ps, i + 1)
                act.copy(xc_t[:, :, i * P:(i + 1) * P],
                         bank[i % 2][:, 0:D].rearrange("p (k s) -> p k s", k=KC)).then_inc(xc_t_ready, 1)
            act.wait_ge(rstd_ready, 2)
            for t in range(NT):
                act.activation(x2_hi[:, t, :], xc[:, t, :], ACT.Copy, scale=rstd[:, t:t + 1]).then_inc(x2_hi_done, 1)
            act.activation(warm[:], std[:], ACT.Gelu)

            def gathered_x(p):
                act.wait_ge(gathered, p + 1)
                act.copy(xt[:], gather_ps()).then_inc(xt_ready, 1)

            def gelu(s):
                act.wait_ge(pre_ready, s + 1)
                act.activation(h_act[:], h_pre[:], ACT.Gelu).then_inc(act_ready, 1)

            def h_transposed(s):
                act.wait_ge(t_done, s + 1)
                act.copy(h_t[:], bank[2].rearrange("p (k s) -> p k s", k=HC)).then_inc(h_t_ready, 1)

            gathered_x(0)
            gelu(0)
            act.wait_ge(experts_ready, 2)
            n_pairs = pairs(act)
            with act.Fori(0, n_pairs) as p:
                h_transposed(p * 2)
                act.wait_ge(up_done, p * 2 + 2)
                gathered_x(p + 1)
                gelu(p * 2 + 1)
                h_transposed(p * 2 + 1)
                gelu(p * 2 + 2)
            with act.If(odd_tile(act) > 0):
                h_transposed(n_pairs * 2)

        @block.vector
        def _(dve):
            n = [0]

            def mark(ins):
                n[0] += 1
                ins.then_inc(vec, 1)

            def wait_marked():
                dve.wait_ge(vec, n[0])

            def chain(ins):
                mark(ins)
                wait_marked()

            def reciprocal_std(round_):
                dve.wait_ge(std_ready, round_)
                chain(dve.reciprocal(rstd[:], std[:]))
                chain(dve.tensor_tensor(newton[:], rstd[:], rstd[:], ALU.mult))
                chain(dve.tensor_tensor(newton[:], newton[:], var_eps[:], ALU.mult))
                chain(dve.tensor_scalar(newton[:], newton[:], -0.5, 1.5, ALU.mult, ALU.add))
                dve.tensor_tensor(rstd[:], rstd[:], newton[:], ALU.mult).then_inc(rstd_ready, 1)
                dve.wait_ge(rstd_ready, round_)

            dve.wait_ge(edges_in, 32)
            dve.tensor_single_scalar(hi_nat[:], src_nat[:], 7, ALU.arith_shift_right).then_inc(vec, 1)
            chain_after = dve.tensor_single_scalar(lo_nat[:], src_nat[:], P - 1, ALU.bitwise_and)
            n[0] += 1
            chain(chain_after)
            dve.tensor_copy(edge_nat[:, 0, :, :], lo_nat[:]).then_inc(edge_nat_done, 1)
            dve.scalar_tensor_tensor(edge_nat[:, 1, :, :], hi_nat[:], float(KEY), dst_nat[:], ALU.mult, ALU.add)\
                .then_inc(edge_nat_done, 1)
            dve.wait_ge(chunks_in, 16)
            chain(dve.tensor_reduce(span[:, 0:1], dst_chunk[:], AX.X, ALU.min))
            chain(dve.tensor_reduce(span[:, 1:2], dst_chunk[:], AX.X, ALU.max))
            dve.wait_ge(consts, 1)
            for i in range(2):
                dve.tensor_scalar(span_diag[:, i, :], ident[0:CHUNKS, 0:CHUNKS], span[:, i:i + 1], None, ALU.mult)\
                    .then_inc(span_ready, 1)
            dve.wait_ge(edge_t_done, 1)
            cols = bank[0][0:EP, 0:2 * ET].rearrange("p (a t) -> p a t", a=2)
            dve.tensor_copy(edge_rel[:, 0, :], cols[:, 0, :]).then_inc(edge_col_done, 1)
            dve.tensor_copy(edge_key[:], cols[:, 1, :]).then_inc(edge_col_done, 1)
            dve.wait_ge(span_ps, 1)
            chain(dve.tensor_copy(span_bc[:], bank[1][:, 0:2 * CHUNKS].rearrange("p (a c) -> p a c", a=2)))

            def set_windows():
                dve.tensor_tensor(edge_rel[:, 1, :].rearrange("p (c i) -> p c i", i=CT),
                                  edge_key[:].rearrange("p (c i) -> p c i", i=CT),
                                  span_bc[0:EP, 0, :].unsqueeze(2).broadcast_to((EP, CHUNKS, CT)), ALU.subtract)
                dve.tensor_copy(base_i[:], span_bc[0:1, 0, :]).then_inc(base_ready, 1)

            set_windows()
            dve.wait_ge(x_in, 32)
            for t in range(NT):
                last = dve.bn_stats(stats[:, t, :], x_sb[:, t, :])
            chain(last)
            for t in range(NT):
                last = dve.bn_aggr(mv[:, t, :], stats[:, t, :])
            chain(last)
            dve.tensor_scalar(var_eps[:], mv[:, :, 1], EPS, None, ALU.add).then_inc(var_ready, 1)
            reciprocal_std(1)
            for t in range(NT):
                dve.tensor_scalar(xn[:, t, :], x_sb[:, t, :], mv[:, t, 0:1], rstd[:, t:t + 1],
                                  ALU.subtract, ALU.mult).then_inc(xn_ready, 1)

            def ys_lower(l, j):
                t = j if l == 0 else YS_ORDER[j]
                dve.wait_ge(ys_hi_done, l * NT + j + 1)
                if l == 0:
                    dve.tensor_tensor(ys_lo[:, t, :], ys_bank(l, j), ys_hi[:, t, :].bitcast(f32),
                                      ALU.subtract).then_inc(ys_ready, 1)
                else:
                    dve.scalar_tensor_tensor(ys_lo[:, t, :], ys_bank(l, j), rdeg_col[:, t:t + 1],
                                             ys_hi[:, t, :].bitcast(f32), ALU.mult, ALU.subtract)\
                        .then_inc(ys_ready, 1)

            for i in range(4):
                cols, c = part(i)
                dve.wait_ge(ht_hi_done, i + 1)
                dve.tensor_tensor(ht_lo[:, c, cols], z_bank(i), ht_hi[:, c, cols].bitcast(f32),
                                  ALU.subtract).then_inc(ht_ready, 1)

            def hot_turn(turn, g):
                dve.tensor_copy(edge_turn[:], edge_rel[:, :, ds(g * (UNROLL * CT), UNROLL * CT)])\
                    .then_inc(turn_ready, 1)
                dve.wait_ge(turn_ready, turn + 1)
                for c in range(0, UNROLL, 2):
                    dve.wait_ge(chunk_free, turn * UNROLL + (c + 2))
                    pair = edge_turn[:, :, c * CT:(c + 2) * CT].rearrange("p a (c i) -> p a c i", i=CT)
                    ring = slice(c % RING, c % RING + 2)
                    dve.tensor_tensor(hot_lo[:, ring, :, :],
                                      iota_lo[0:EP].unsqueeze(1).broadcast_to((EP, 2, P, CT)),
                                      pair[:, 0].unsqueeze(2).broadcast_to((EP, 2, P, CT)), ALU.is_equal)
                    dve.tensor_tensor(hot_key[:, ring, :, :],
                                      iota_key[0:EP].unsqueeze(1).broadcast_to((EP, 2, NT * WD, CT)),
                                      pair[:, 1].unsqueeze(2).broadcast_to((EP, 2, NT * WD, CT)), ALU.is_equal)\
                        .then_inc(hot_chunk, 2)
                dve.wait_ge(hot_chunk, turn * UNROLL + UNROLL)

            dve.wait_ge(base_ready, 1)
            dve.wait_ge(edge_col_done, 2)
            for i in range(len(SEGMENTS) - 1):
                with dve.Fori(SEGMENTS[i], SEGMENTS[i + 1]) as g:
                    hot_turn(g, g)
                if i >= 2:
                    for t in SEG_TILES[i - 2]:
                        ys_lower(0, t)
            chain(dve.tensor_tensor(shared[:], span_bc[0:1, 1, 0:CHUNKS - 2], span_bc[0:1, 0, 2:], ALU.is_ge))
            chain(dve.tensor_reduce(any_shared[:], shared[:], AX.X, ALU.max))
            chain(dve.tensor_tensor(width[:], span_bc[0:1, 1, :], span_bc[0:1, 0, :], ALU.subtract))
            chain(dve.tensor_reduce(widest[:], width[:], AX.X, ALU.max))
            dve.wait_ge(consts, 4)
            chain(dve.tensor_scalar(needed[:], steps[:], widest[:], None, ALU.is_le))
            chain(dve.tensor_reduce(meta[:, 0:1], needed[:], AX.X, ALU.add))
            chain(dve.scalar_tensor_tensor(meta[:, 1:2], meta[:, 0:1], 1.0, any_shared[:], ALU.is_gt, ALU.max))
            chain(dve.tensor_scalar(meta[:, 0:1], meta[:, 0:1], 1.0, None, ALU.add))
            dve.tensor_copy(meta_i[:], meta[:]).then_inc(meta_ready, 1)
            dve.wait_ge(meta_ready, 1)
            with dve.If(general(dve) > 0):
                with dve.Fori(1, pass_end(dve)) as v:
                    dve.wait_ge(a_written, v * CHUNKS + 2)
                    dve.sem_inc(pass_begun, 1)
                    with dve.If(v < 2):
                        dve.memset(a_f[:], 0.0).then_inc(a_zeroed, 1)
                        dve.wait_ge(a_zeroed, 3)
                    set_windows()
                    dve.wait_ge(base_ready, v + 1)
                    dve.sem_inc(pass_begun, 1)
                    with dve.Fori(0, TURNS) as g:
                        hot_turn(v * TURNS + g, g)
                    dve.tensor_scalar(span_bc[:, 0, :], span_bc[:, 0, :], float(WD), float(NPAD),
                                      ALU.add, ALU.min).then_inc(window_moved, 1)
                    dve.wait_ge(window_moved, v)

            dve.wait_ge(a_complete, 1)
            for u, cols in DVE_ADDS:
                dve.tensor_tensor(a_hi[:, u, cols], a_hi[:, u, cols].bitcast(f32), a_f[:, u, cols], ALU.add)\
                    .then_inc(a_added, 1)
            for t in SEG_TILES[-2] + SEG_TILES[-1]:
                ys_lower(0, t)
            dve.wait_ge(cnt_done, 1)
            dve.tensor_copy(cnt_f[:], cnt_ps[:, 0:NPAD]).then_inc(cnt_read, 1)
            dve.wait_ge(cnt_read, 1)
            dve.wait_ge(h0_copied, 4)
            for c in range(KC):
                dve.tensor_tensor(ht_f[:, c, :], ht_f[:, c, :], cnt_f[:], ALU.mult).then_inc(u0_ready, 1)
            for j, i in enumerate(Z_ORDER):
                cols, c = part(i)
                dve.wait_ge(ut_hi_done, j + 1)
                dve.tensor_tensor(ut_lo[:, c, cols], ht_f[:, c, cols], ut_hi[:, c, cols].bitcast(f32),
                                  ALU.subtract).then_inc(ut_ready, 1)
            chain(dve.tensor_tensor(diag[:], cnt_f[:].rearrange("p (t m) -> p t m", t=NT),
                                    ident[:].unsqueeze(1).broadcast_to((P, NT, P)), ALU.mult))
            chain(dve.tensor_reduce(deg_col[:], diag[:], AX.X, ALU.add))
            chain(dve.tensor_scalar(deg_col[:], deg_col[:], 1.0, None, ALU.max))
            dve.reciprocal(rdeg_col[:], deg_col[:]).then_inc(rdeg_ready, 1)
            dve.wait_ge(rdeg_ready, 1)
            dve.tensor_tensor(diag[:], rdeg_col[:].unsqueeze(2).broadcast_to((P, NT, P)),
                              ident[:].unsqueeze(1).broadcast_to((P, NT, P)), ALU.mult).then_inc(rdeg_ready, 1)

            for l in range(LEVELS):
                if l == 0:
                    dve.wait_ge(ut_ready, 4)
                else:
                    dve.wait_ge(ht_ready, 4 * (l + 1))
                for j, i in enumerate(Z_ORDER):
                    cols, c = part(i)
                    if l < LEVELS - 1:
                        dve.wait_ge(ut_hi_done, 4 * (l + 1) + j + 1)
                        dve.scalar_tensor_tensor(ut_lo[:, c, cols], z_bank(i), 0.0, ut_hi[:, c, cols].bitcast(f32),
                                                 ALU.max, ALU.subtract).then_inc(ut_ready, 1)
                    else:
                        dve.wait_ge(z_done, 4 * l + j + 1)
                    if l == 0 and j == 0:
                        dve.wait_ge(rdeg_ps, 1)
                        dve.tensor_copy(rdeg[:, 0:HALVES[0][1]], rdeg_bank(0)).then_inc(rdeg_ready, 1)
                        dve.tensor_copy(rdeg[:, HALVES[0][1]:], rdeg_bank(1)).then_inc(rdeg_ready, 1)
                        dve.wait_ge(rdeg_ready, 4)
                    dve.scalar_tensor_tensor(ht_f[:, c, cols], z_bank(i), 0.0, rdeg[:, cols],
                                             ALU.max, ALU.mult).then_inc(ht_f_done, 1)
                if l < LEVELS - 1:
                    for j in range(NT):
                        ys_lower(l + 1, j)
                for j, i in enumerate(Z_ORDER):
                    cols, c = part(i)
                    dve.wait_ge(ht_hi_done, 4 * (l + 1) + j + 1)
                    hi, lo = (ht_hi, ht_lo) if l < LEVELS - 1 else (ut_hi, ut_lo)
                    dve.tensor_tensor(lo[:, c, cols], ht_f[:, c, cols], hi[:, c, cols].bitcast(f32),
                                      ALU.subtract).then_inc(ht_ready, 1)

            G_ORDER = (4, 0, 1, 2, 3)
            for t in G_ORDER:
                same_bank = [u for u in range(NT) if u // 2 == t // 2]
                dve.wait_ge(g_done, max(YS_ORDER.index(u) + 1 for u in same_bank))
                dve.tensor_tensor(x1_sb[:, t, :], g_tile(t), x_sb[:, t, :], ALU.add).then_inc(x1_ready, 1)
                n_x1 = G_ORDER.index(t) + 1
                if n_x1 in (1, 3, NT):
                    dve.wait_ge(x1_ready, n_x1)
                    for u in G_ORDER[max(n_x1 - 2, 0):n_x1]:
                        last = dve.bn_stats(stats[:, u, :], x1_sb[:, u, :])
            chain(last)
            for t in range(NT):
                last = dve.bn_aggr(mv[:, t, :], stats[:, t, :])
            chain(last)
            dve.tensor_scalar(var_eps[:], mv[:, :, 1], EPS, None, ALU.add).then_inc(var_ready, 1)
            for t in range(NT):
                dve.tensor_scalar(xc[:, t, :], x1_sb[:, t, :], mv[:, t, 0:1], None, ALU.subtract).then_inc(xc_ready, 1)
            reciprocal_std(2)
            dve.wait_ge(xc_ready, NT)
            dve.wait_ge(ffn_w_in, 16 * (2 + 2 * EXPERTS))
            dve.wait_ge(ffn_consts, 8)
            chain(dve.tensor_scalar(valid[:], node_id[:], float(NODES), None, ALU.is_lt))
            chain(dve.tensor_tensor(row_id[:], row_id[:], valid[:], ALU.mult))
            for t in range(NT):
                dve.wait_ge(x2_hi_done, t + 1)
                dve.scalar_tensor_tensor(x2_lo[:, t, :], xc[:, t, :], rstd[:, t:t + 1], x2_hi[:, t, :].bitcast(f32),
                                         ALU.mult, ALU.subtract).then_inc(x2_lo_done, 1)
            dve.wait_ge(score_ps, 1)
            tokens = (P, NT, EXPERTS)
            chain(dve.tensor_tensor(score[:], bank[4][:, 0:NT * EXPERTS].rearrange("p (t e) -> p t e", t=NT),
                                    rstd[:].unsqueeze(2).broadcast_to(tokens), ALU.mult))
            chain(dve.tensor_tensor(score[:], score[:], bg_bc[:].unsqueeze(1).broadcast_to(tokens), ALU.add))
            for t in range(NT):
                last = dve.max(best[:, t, :], score[:, t, :])
            chain(last)
            for t in range(NT):
                last = dve.max_index(best_id[:, t, :], best[:, t, :], score[:, t, :])
            chain(last)
            for k in range(2):
                last = dve.tensor_tensor(pick[:, k, :, :], iota_e[:], best_id[:, :, k:k + 1].broadcast_to((P, NT, EXPERTS)),
                                         ALU.is_equal)
            chain(last)
            chain(dve.tensor_tensor(both[:], pick[:, 0, :, :], pick[:, 1, :, :], ALU.add))
            dve.tensor_tensor(both_bf[:], both[:], valid[:].unsqueeze(2).broadcast_to((P, NT, EXPERTS)), ALU.mult)\
                .then_inc(both_ready, 1)
            dve.wait_ge(prefix_ps, 1)
            total = bank[4][:, 128:128 + EXPERTS]
            before = bank[4][:, 256:256 + NT * EXPERTS].rearrange("p (t e) -> p t e", t=NT)
            chain(dve.tensor_scalar(tiles_i[:, 0, :], total, float(P - 1), None, ALU.add))
            chain(dve.tensor_single_scalar(tiles_i[:, 1, :], tiles_i[:, 0, :], 7, ALU.arith_shift_right))
            chain(dve.tensor_copy(tiles_f[:], tiles_i[:, 1, :]))
            chain(dve.tensor_tensor_scan(tiles_end[:], tiles_f[:], zeros_e[:], 0.0, ALU.add, ALU.add))

            spread_e = (1, SLOT_TILES, EXPERTS)
            spread = (P, 2, SLOT_TILES, NT)
            mark(dve.tensor_tensor(slot0[:], tiles_end[:], tiles_f[:], ALU.subtract))
            dve.tensor_tensor(past[:], iota_s[0:1].unsqueeze(2).broadcast_to(spread_e),
                              tiles_end[0:1, :].unsqueeze(1).broadcast_to(spread_e), ALU.is_ge)
            wait_marked()
            mark(dve.scalar_tensor_tensor(slot[:], slot0[:].unsqueeze(1).broadcast_to((P, NT, EXPERTS)), float(P),
                                          before, ALU.mult, ALU.add))
            dve.tensor_copy(owner[:, SLOT_TILES:], tiles_end[0:1, EXPERTS - 1:EXPERTS])
            wait_marked()
            for k in range(2):
                last = dve.tensor_tensor(slot_pick[:, k, :, :], pick[:, k, :, :], slot[:], ALU.mult)
            mark(last)
            dve.tensor_reduce(owner[:, 0:SLOT_TILES], past[:], AX.X, ALU.add)
            wait_marked()
            chain(dve.tensor_reduce(slot_of[:], slot_pick[:], AX.X, ALU.add))
            dve.tensor_copy(slot_i[:], slot_of[:])
            mark(dve.scalar_tensor_tensor(slot_1[:], slot_of[:], 1.0, valid[:].unsqueeze(1).broadcast_to((P, 2, NT)),
                                          ALU.add, ALU.mult))
            dve.tensor_scalar(owner[:, 0:SLOT_TILES], owner[:, 0:SLOT_TILES], float(EXPERTS - 1), None, ALU.min)
            wait_marked()
            mark(dve.tensor_tensor(from_tile[:], slot_1[:].unsqueeze(2).broadcast_to(spread),
                                   tile_start[:].unsqueeze(1).broadcast_to(spread), ALU.subtract))
            dve.tensor_single_scalar(pos_i[:], slot_i[:], P - 1, ALU.bitwise_and)
            wait_marked()
            mark(dve.scalar_tensor_tensor(in_tile[:], from_tile[:], float(P), from_tile[:], ALU.is_le, ALU.mult))
            dve.tensor_copy(owner_i[:], owner[:])
            wait_marked()
            mark(dve.tensor_tensor(hot_pos[:], in_tile[:, 0], in_tile[:, 1], ALU.max))
            dve.tensor_scalar(pos_f[:], pos_i[:], 1.0, None, ALU.add)
            wait_marked()

            def take_pair(p):
                dve.tensor_copy(pair_pos[:], hot_pos[:, ds(p * 2, 2), :]).then_inc(pair_taken, 1)

            def one_hot(p, place):
                for h in range(2):
                    last = dve.tensor_tensor(hot_slot[:, :, h * P:(h + 1) * P],
                                             iota_p[:].unsqueeze(1).broadcast_to((P, NT, P)),
                                             place[:, h, :].unsqueeze(2).broadcast_to((P, NT, P)), ALU.is_equal)
                last.then_inc(hot_ready, 1)
                dve.wait_ge(hot_ready, p + 1)

            def add_b1(s, e):
                dve.wait_ge(up_done, s + 1)
                dve.wait_ge(act_ready, s)
                dve.tensor_tensor(h_pre[:], bank[1][:, :], b1_bc[:, ds(e, 1), :], ALU.add).then_inc(pre_ready, 1)

            def add_b2(s, h, e):
                dve.wait_ge(y_landed, s + 1)
                dve.wait_ge(down_done, s + 1)
                dve.tensor_tensor(y_sb[:, h, :], bank[3][:, 0:D], b2_bc[:, ds(e, 1), :], ALU.add).then_inc(y_ready, 1)

            one_hot(0, hot_pos[:, 0:2, :])
            dve.tensor_single_scalar(pairs_i[:, 0:1], owner_i[:, SLOT_TILES:], 1, ALU.arith_shift_right)\
                .then_inc(experts_ready, 1)
            dve.tensor_single_scalar(pairs_i[:, 1:2], owner_i[:, SLOT_TILES:], 1, ALU.bitwise_and)\
                .then_inc(experts_ready, 1)
            dve.tensor_tensor(hot_place[:].rearrange("p k t m -> p (k t) m"),
                              iota_p[:].unsqueeze(1).broadcast_to((P, 2 * NT, P)),
                              pos_f[:].rearrange("p k t -> p (k t)").unsqueeze(2).broadcast_to((P, 2 * NT, P)),
                              ALU.is_equal)

            def row_of_tile(k):
                return dve.scalar_tensor_tensor(row_in_tile[:, k], in_tile[:, k], 0.0,
                                                row_id[:].unsqueeze(1).broadcast_to((P, SLOT_TILES, NT)),
                                                ALU.is_gt, ALU.mult)

            row_of_tile(0)
            row_of_tile(1).then_inc(row_pairs_ready, 1)
            dve.wait_ge(gathered, 1)
            one_hot(1, hot_pos[:, 2:4, :])
            dve.wait_ge(experts_ready, 2)
            dve.wait_ge(ffn_b_in, 16 * (EXPERTS + 1))
            e = expert_of(dve, 0)
            dve.wait_ge(up_done, 1)
            dve.tensor_tensor(h_pre[:], bank[1][:, :], b1_bc[:, ds(e, 1), :], ALU.add).then_inc(pre_ready, 1)
            dve.wait_ge(row_ps, 1)
            rows_1 = bank[4][:, 0:SLOT_TILES]
            chain(dve.tensor_scalar(unused[:], rows_1, 0.0, spare_row[:], ALU.is_equal, ALU.mult))
            dve.scalar_tensor_tensor(row_of[:], rows_1, -1.0, unused[:], ALU.add, ALU.add).then_inc(rows_ready, 1)
            dve.sem_inc(y_ready, 1)
            n_pairs = pairs(dve)
            with dve.Fori(0, n_pairs) as p:
                a, b = p * 2, p * 2 + 1
                e_b = expert_of(dve, b)
                e_a = expert_of(dve, a)
                add_b1(b, e_b)
                take_pair(p + 2)
                dve.wait_ge(gathered, p + 2)
                dve.wait_ge(pair_taken, p + 1)
                one_hot(p + 2, pair_pos)
                add_b2(a, 0, e_a)
                add_b1(b + 1, expert_of(dve, b + 1))
                add_b2(b, 1, e_b)
            with dve.If(odd_tile(dve) > 0):
                s = n_pairs * 2
                add_b2(s, 0, expert_of(dve, s))

        @block.tensor
        def _(pe):
            def exact3(out_, lhs, rhs, first, last):
                (lh, ll), (rh, rl) = lhs, rhs
                pe.matmul(out_, lh, rh, start=first, stop=False, skip_group_check=True)
                pe.matmul(out_, lh, rl, start=False, stop=False, skip_group_check=True)
                return pe.matmul(out_, ll, rh, start=False, stop=last, skip_group_check=True)

            def keep_busy(n, free=3):
                for _ in range(n):
                    pe.matmul(bank[free][:, 0:P], ident[:], ident[:], start=True, stop=True)

            pe.wait_ge(consts, 1)
            pe.wait_ge(edge_nat_done, 2)
            for a in range(2):
                for j in range(EH):
                    o = a * ET + j * EQ
                    last = pe.transpose(bank[0][0:EP, o:o + EQ], edge_nat[:, a, j, :], ident[0:EQ, 0:EQ])
            last.then_inc(edge_t_done, 1)
            pe.wait_ge(consts, 5)
            pe.wait_ge(span_ready, 2)
            pe.matmul(bank[1][:, 0:2 * CHUNKS], ones_sq[0:CHUNKS, :].bitcast(f32),
                      span_diag[:].rearrange("q a c -> q (a c)"), start=True, stop=True).then_inc(span_ps, 1)
            pe.wait_ge(edge_t_done, 1)
            for i, (h, c) in enumerate(Z_OUT):
                a, b = HALVES[h]
                if i == 0:
                    pe.wait_ge(edge_col_done, 2)
                if i == 1:
                    pe.wait_ge(base_ready, 1)
                for t in range(a // P, b // P):
                    pe.wait_ge(xn_ready, t + 1)
                    last = pe.transpose(bank[i][:, t * P - a:(t + 1) * P - a], xn[:, t, c * P:(c + 1) * P], ident[:])
                last.then_inc(xn_t_done, 1)

            def ys_product(l, j):
                t = j if l == 0 else YS_ORDER[j]
                r, cols, o = l % 2, slice(t * P, (t + 1) * P), ys_bank(l, j)
                (hi, lo) = (ht_hi, ht_lo) if l == 0 else (ut_hi, ut_lo)
                for k in range(KC):
                    last = exact3(o, (hi[:, k, cols], lo[:, k, cols]),
                                  (w_hi[:, r, k, 0:D], w_lo[:, r, k, 0:D]), k == 0, k == KC - 1)
                last.then_inc(ys_done, 1)

            def g_product(l, t, hi=ht_hi, lo=ht_lo):
                r, cols = l % 2, slice(t * P, (t + 1) * P)
                for k in range(KC):
                    last = exact3(g_tile(t), (hi[:, k, cols], lo[:, k, cols]),
                                  (w_hi[:, r, k, 2 * D:], w_lo[:, r, k, 2 * D:]), False,
                                  l == LEVELS and k == KC - 1)
                return last

            pe.wait_ge(b_ready, 2)
            for t in range(NT):
                pe.matmul(g_tile(t), row_pick[:, LEVELS, :], b_split[:], start=t % 2 == 0, stop=False,
                          skip_group_check=True)

            def sum_turn(turn, g, add_to=None):
                for c in range(UNROLL):
                    if add_to is not None:
                        start = window_start(pe, g * UNROLL + c)
                    pe.wait_ge(a_written, turn * UNROLL + (c + 1))
                    if c % 2 == 0:
                        pe.wait_ge(hot_chunk, turn * UNROLL + (c + 2))
                    for i in range(CT):
                        last = pe.matmul(bank[c % 2][:, 0:NT * WD], hot_lo[:, c % RING, :, i], hot_key[:, c % RING, :, i],
                                         start=i == 0, stop=add_to is None and i == CT - 1, skip_group_check=True)
                    last.then_inc(chunk_free, 1)
                    if add_to is not None:
                        pe.wait_ge(a_written, turn * UNROLL + (c + 2))
                        pe.matmul(pane(c), ident[:], add_to[:, :, ds(start, WD)], start=False, stop=True,
                                  skip_group_check=True).then_inc(chunk_done, 1)

            pe.wait_ge(consts, 7)
            pe.wait_ge(base_ready, 1)
            pe.wait_ge(ht_ready, 4)
            pe.sem_inc(chunk_free, RING)
            for i in range(len(SEGMENTS) - 1):
                with pe.Fori(SEGMENTS[i], SEGMENTS[i + 1]) as g:
                    sum_turn(g, g)
                if i == 0:
                    pe.wait_ge(w_split, 1)
                for t in SEG_TILES[i]:
                    if t >= 3:
                        pe.wait_ge(ys_ready, t - 2)
                    ys_product(0, t)
            for t in range(NT):
                last = g_product(0, t)
            last.then_inc(g_added, 1)
            pe.wait_ge(a_written, TURNS * UNROLL + 2)
            keep_busy(WARM_DEGREE, 0)
            pe.wait_ge(meta_ready, 1)
            is_general = general(pe)
            with pe.If(is_general > 0):
                with pe.Fori(1, pass_end(pe)) as v:
                    pe.wait_ge(base_ready, v + 1)
                    pe.sem_inc(pass_begun, 1)
                    with pe.Fori(0, TURNS) as g:
                        sum_turn(v * TURNS + g, g, add_to=a_f)
            pe.wait_ge(a_complete, 1)
            pe.wait_ge(ys_ready, NT)
            parts = [slice(0, 512), slice(512, NPAD)]

            def degrees(ones, a_t):
                for u in range(NT):
                    pe.wait_ge(a_added, min(u + 1, NT - 1))
                    if u >= NT - 2:
                        pe.wait_ge(a_added_pool, 2)
                    for cols in parts:
                        last = pe.matmul(cnt_ps[:, cols], ones, a_t[:, u, cols], start=u == 0, stop=u == NT - 1,
                                         skip_group_check=True)
                last.then_inc(cnt_done, 1)

            with pe.If(is_general > 0):
                degrees(ones_sq[:].bitcast(f32), a_f)
            with pe.Else():
                degrees(ones_sq[:], a_hi)

            def gathered_sum(l, i, y_parts, a_t, first, last):
                cols, c = part(i)
                m = slice(c * P, (c + 1) * P)
                for u in range(NT):
                    for y in y_parts:
                        step = pe.matmul(z_bank(i), y[:, u, m], a_t[:, u, cols],
                                         start=first and u == 0 and y is y_parts[0],
                                         stop=last and u == NT - 1 and y is y_parts[-1], skip_group_check=True)
                if last:
                    step.then_inc(z_done, 1)

            def own_part(l, i, bias, cnt, first, last):
                cols, c = part(i)
                m = slice(c * P, (c + 1) * P)
                pe.matmul(z_bank(i), bias[:, l, m], cnt[:, cols], start=first, stop=False, skip_group_check=True)
                for k in range(KC):
                    step = exact3(z_bank(i), (w_hi[:, l % 2, k, D + c * P:D + (c + 1) * P],
                                              w_lo[:, l % 2, k, D + c * P:D + (c + 1) * P]),
                                  (ut_hi[:, k, cols], ut_lo[:, k, cols]), False, last and k == KC - 1)
                if last and c == KC - 1:
                    step.then_inc(z_done, KC)

            def add_h(l):
                pe.wait_ge(ht_ready, 4 * (l + 1))
                for t in range(NT):
                    step = g_product(l, t)
                step.then_inc(g_added, 1)

            def level_sums(l, y_parts, a_t, bias, cnt):
                if l == 0:
                    pe.wait_ge(ys_ready, NT)
                    for i in range(4):
                        if i == 2:
                            pe.wait_ge(cnt_read, 2)
                        gathered_sum(l, i, y_parts, a_t, True, False)
                    pe.wait_ge(ut_ready, 4)
                    for i in Z_ORDER[:2]:
                        own_part(l, i, bias, cnt, False, True)
                    pe.wait_ge(rdeg_ready, 2)
                    flat = diag[:].rearrange("p t m -> p (t m)")
                    pe.matmul(rdeg_bank(0), ones_sq[:].bitcast(f32), flat[:, slice(*HALVES[0])], start=True, stop=True,
                              skip_group_check=True)
                    pe.matmul(rdeg_bank(1), ones_sq[:].bitcast(f32), flat[:, slice(*HALVES[1])], start=False, stop=True,
                              skip_group_check=True).then_inc(rdeg_ps, 1)
                    for i in Z_ORDER[2:]:
                        own_part(l, i, bias, cnt, False, True)
                else:
                    pe.wait_ge(ut_ready, 4 * l + 2)
                    pe.wait_ge(ht_f_done, 4 * (l - 1) + 2)
                    own_part(l, 2, bias, cnt, True, False)
                    own_part(l, 3, bias, cnt, True, False)
                    pe.wait_ge(rdeg_ready, 4)
                    for j in range(NT):
                        if j == 1:
                            pe.wait_ge(ht_f_done, 4 * l)
                        if j == YS_ORDER.index(0):
                            pe.wait_ge(ut_ready, 4 * l + 4)
                        if j >= 3:
                            pe.wait_ge(ys_ready, l * NT + j - 2)
                        ys_product(l, j)
                    pe.wait_ge(ys_ready, l * NT + 3)
                    own_part(l, 1, bias, cnt, True, False)
                    pe.wait_ge(ys_ready, (l + 1) * NT)
                    own_part(l, 0, bias, cnt, True, False)
                    for i in (2, 3):
                        gathered_sum(l, i, y_parts, a_t, False, True)
                    if l < LEVELS - 1:
                        add_h(l)
                    for i in (0, 1):
                        gathered_sum(l, i, y_parts, a_t, False, True)

            for l in range(LEVELS):
                if l:
                    pe.wait_ge(w_split, l + 1)
                with pe.If(is_general > 0):
                    level_sums(l, [ys_hi[:].bitcast(f32), ys_lo[:].bitcast(f32)], a_f, b_level[:].bitcast(f32),
                               cnt_f[0:BR, :])
                with pe.Else():
                    level_sums(l, [ys_hi, ys_lo], a_hi, b_level, cnt_r)
            add_h(LEVELS - 1)
            pe.wait_ge(w_split, LEVELS + 1)
            for j, t in enumerate(YS_ORDER):
                if j in (0, 2):
                    pe.wait_ge(ht_ready, 4 * LEVELS + (4 if j else 2))
                g_product(LEVELS, t, ut_hi, ut_lo).then_inc(g_done, 1)

            keep_busy(WARM_NORM)
            for t in range(NT):
                pe.wait_ge(xc_ready, t + 1)
                if t >= 2:
                    pe.wait_ge(xc_t_ready, t - 1)
                for k in range(KC):
                    last = pe.transpose(bank[t % 2][:, k * P:(k + 1) * P], xc[:, t, k * P:(k + 1) * P], ident[:])
                last.then_inc(xc_t_ps, 1)
            keep_busy(WARM_GATE)
            pe.wait_ge(ffn_w_in, 16 * (2 + 2 * EXPERTS))
            for t in range(NT):
                pe.wait_ge(xc_t_ready, t + 1)
                o = bank[4][:, t * EXPERTS:(t + 1) * EXPERTS]
                for k in range(KC):
                    last = pe.matmul(o, xc_t[:, k, t * P:(t + 1) * P], wg_sb[:, k, :], start=k == 0, stop=k == KC - 1,
                                     skip_group_check=True)
            last.then_inc(score_ps, 1)
            keep_busy(WARM_ROUTE)
            pe.wait_ge(both_ready, 1)
            total, before = bank[4][:, 128:128 + EXPERTS], bank[4][:, 256:256 + NT * EXPERTS]
            pe.matmul(before, tri_bf[:], both_bf[:].rearrange("p t e -> p (t e)"), start=True, stop=False,
                      skip_group_check=True)
            for j in range(1, NT):
                pe.matmul(before[:, j * EXPERTS:], ones_bf[:], both_bf[:, 0:NT - j, :].rearrange("p t e -> p (t e)"),
                          start=False, stop=j == NT - 1, skip_group_check=True)
            for t in range(NT):
                last = pe.matmul(total, ones_bf[:], both_bf[:, t, :], start=False, stop=t == NT - 1,
                                 skip_group_check=True)
            last.then_inc(prefix_ps, 1)

            def gather(p):
                pe.wait_ge(hot_ready, p + 1)
                for k in range(KC):
                    o = bank[0][:, k * 2 * P:(k + 1) * 2 * P]
                    for t in range(NT):
                        pe.matmul(o, x2_hi[:, t, k * P:(k + 1) * P], hot_slot[:, t, :], start=t == 0 and k == 0,
                                  stop=False, skip_group_check=True)
                        last = pe.matmul(o, x2_lo[:, t, k * P:(k + 1) * P], hot_slot[:, t, :], start=False,
                                         stop=t == NT - 1, skip_group_check=True)
                last.then_inc(gathered, 1)

            def up(h, e):
                for k in range(KC):
                    last = pe.matmul(bank[1][:, :], xt[:, k, h * P:(h + 1) * P], w1_sb[:, ds(e, 1), k, :],
                                     start=k == 0, stop=k == KC - 1)
                last.then_inc(up_done, 1)

            def transpose_h(s):
                pe.wait_ge(act_ready, s + 1)
                for k in range(HC):
                    last = pe.transpose(bank[2][:, k * P:(k + 1) * P], h_act[:, k * P:(k + 1) * P], ident[:])
                last.then_inc(t_done, 1)

            def down(s, e):
                pe.wait_ge(y_ready, s + 1)
                pe.wait_ge(h_t_ready, s + 1)
                for k in range(HC):
                    last = pe.matmul(bank[3][:, 0:D], h_t[:, k, :], w2_sb[:, ds(e, 1), k, :], start=k == 0,
                                     stop=k == HC - 1)
                last.then_inc(down_done, 1)

            keep_busy(WARM_GATHER)
            pe.wait_ge(x2_lo_done, NT)
            gather(0)
            pe.wait_ge(row_pairs_ready, 1)
            for k in range(2):
                for t in range(NT):
                    last = pe.matmul(bank[4][:, 0:SLOT_TILES], hot_place[:, k, t, :], row_in_tile[:, k, :, t],
                                     start=k == 0 and t == 0, stop=k == 1 and t == NT - 1)
            last.then_inc(row_ps, 1)
            pe.wait_ge(experts_ready, 2)
            e = expert_of(pe, 0)
            pe.wait_ge(xt_ready, 1)
            up(0, e)
            n_pairs = pairs(pe)
            with pe.Fori(0, n_pairs) as p:
                a, b = p * 2, p * 2 + 1
                gather(p + 1)
                e_a = expert_of(pe, a)
                transpose_h(a)
                e_b = expert_of(pe, b)
                up(1, e_b)
                e_next = expert_of(pe, b + 1)
                down(a, e_a)
                transpose_h(b)
                pe.wait_ge(xt_ready, p + 2)
                up(0, e_next)
                down(b, e_b)
            with pe.If(odd_tile(pe) > 0):
                s = n_pairs * 2
                transpose_h(s)
                down(s, expert_of(pe, s))


_INS = ["x", "src", "dst"] + [f"L0_gnn_{n}" for n in ("W0", "b0", "W1", "b1", "W2", "b2", "Wf", "bf")] \
    + [f"L0_ffn_{n}" for n in ("Wg", "bg", "W1", "b1", "W2", "b2")]


def kernel(**inputs):
    import concourse.bacc as bacc
    from concourse.bass_utils import run_bass_kernel_spmd

    nc = bacc.Bacc("TRN2", target_bir_lowering=False, num_devices=1)
    arrays, ap = {}, {}
    for name in _INS:
        a = np.ascontiguousarray(inputs[name])
        arrays[f"in_{name}"] = a
        ap[name] = nc.dram_tensor(f"in_{name}", a.shape, mybir.dt.from_np(a.dtype), kind="ExternalInput").ap()
    out = nc.dram_tensor("out_rows", (SPARE + P, D), mybir.dt.float32, kind="ExternalOutput").ap()
    g = {n: ap[f"L0_gnn_{n}"] for n in ("W0", "b0", "W1", "b1", "W2", "b2", "Wf", "bf")}
    f = {n: ap[f"L0_ffn_{n}"] for n in ("Wg", "bg", "W1", "b1", "W2", "b2")}
    build(nc, ap["x"], ap["src"], ap["dst"], [g["W0"], g["W1"], g["W2"]], [g["b0"], g["b1"], g["b2"]],
          g["Wf"], g["bf"], f["Wg"], f["bg"], f["W1"], f["b1"], f["W2"], f["b2"], out)
    r = run_bass_kernel_spmd(nc, [arrays], core_ids=[0])
    return r.results[0]["out_rows"][:NODES]
```
